# Optimizing a Trainium2 kernel written in Bass

```python
import numpy as np
import jax
import jax.numpy as jnp

def _softmax(x, axis=-1):
    return jax.nn.softmax(x, axis=axis)

def _gelu(x):
    return jax.nn.gelu(x, approximate=True)

def _silu(x):
    return jax.nn.silu(x)

def _sigmoid(x):
    return jax.nn.sigmoid(x)

def _layernorm(x, axis=-1, eps=1e-05):
    m = jnp.mean(x, axis=axis, keepdims=True)
    v = jnp.var(x, axis=axis, keepdims=True)
    return (x - m) / jnp.sqrt(v + eps)

def _scatter_add(tgt, idx, src, axis=0):
    return tgt.at[idx].add(src)

def _segment_sum(src, seg, n):
    return jax.ops.segment_sum(src, seg, n)
kernel_name = 'mk_gnn_preln_d2_gnn_r8_7e9b3a'

def setup_inputs(seed: int=0):
    np.random.seed(seed)
    _w = jnp.asarray

    def _rec_inputs():
        import jax
        import jax.numpy as jnp
        _gk = jax.random.key(seed)
        x = -0.0001006 + 1 * jax.random.normal(jax.random.fold_in(_gk, 1), (6250, 96), jnp.float32)
        _s = jax.random.randint(jax.random.fold_in(_gk, 2), (50000,), 0, 6250, jnp.int32)
        _d = jax.random.randint(jax.random.fold_in(_gk, 3), (50000,), 0, 6250, jnp.int32)
        _loop = jnp.arange(6250, dtype=jnp.int32)
        src = jnp.concatenate([_s, _d, _loop])
        dst = jnp.concatenate([_d, _s, _loop])
        _o = jnp.argsort(dst, stable=True)
        src = src[_o]
        dst = dst[_o]
        edge_attr_32 = 0.000196303 + 1.00016 * jax.random.normal(jax.random.fold_in(_gk, 11), (106250, 32), jnp.float32)
        return (x, src, dst, edge_attr_32)
    x, src, dst, edge_attr_32 = _rec_inputs()

    def _L0_gnn_setup():
        import jax, jax.numpy as jnp
        import numpy as np
        N, E = (6250, 100000)
        ND, ED = (96, 32)

        def _gelu(x):
            return jax.nn.gelu(x, approximate=False)
        key = jax.random.key(seed)
        ks = jax.random.split(key, 16)
        s = lambda fan_in: 1.0 / np.sqrt(fan_in)
        inp = {'x': jax.random.normal(ks[0], (N, ND), jnp.float32), 'edge_index': jax.random.randint(ks[1], (2, E), 0, N, jnp.int32), 'edge_attr': jax.random.normal(ks[2], (E, ED), jnp.float32), 'mW1': jax.random.uniform(ks[3], (ND + ED, ND), jnp.float32, -s(ND + ED), s(ND + ED)), 'mb1': jnp.zeros((ND,), jnp.float32), 'mW2': jax.random.uniform(ks[4], (ND, ND), jnp.float32, -s(ND), s(ND)), 'mb2': jnp.zeros((ND,), jnp.float32), 'gW1': jax.random.uniform(ks[5], (ND + ED, ND), jnp.float32, -s(ND + ED), s(ND + ED)), 'gb1': jnp.zeros((ND,), jnp.float32), 'gW2': jax.random.uniform(ks[6], (ND, 1), jnp.float32, -s(ND), s(ND)), 'gb2': jnp.zeros((1,), jnp.float32), 'uW1': jax.random.uniform(ks[7], (2 * ND, ND), jnp.float32, -s(2 * ND), s(2 * ND)), 'ub1': jnp.zeros((ND,), jnp.float32), 'uW2': jax.random.uniform(ks[8], (ND, ND), jnp.float32, -s(ND), s(ND)), 'ub2': jnp.zeros((ND,), jnp.float32), 'ln_g': jnp.ones((ND,), jnp.float32), 'ln_b': jnp.zeros((ND,), jnp.float32)}
        return inp
    _L0_gnn_all = _L0_gnn_setup()
    _L0_gnn_in = {k: v for k, v in _L0_gnn_all.items() if k in ('mW1', 'mb1', 'mW2', 'mb2', 'gW1', 'gb1', 'gW2', 'gb2', 'uW1', 'ub1', 'uW2', 'ub2', 'ln_g', 'ln_b')}
    del _L0_gnn_all

    def _L1_gnn_setup():
        import jax, jax.numpy as jnp
        import numpy as np
        N_NODES = 12500
        N_EDGES = 100000
        D = 96
        BN_EPS = 1e-05
        LEAKY_SLOPE = 0.01

        def _batch_norm(h, gamma, beta):
            mu = h.mean(axis=0)
            var = jnp.mean(jnp.square(h - mu), axis=0)
            return gamma * (h - mu) * jax.lax.rsqrt(var + BN_EPS) + beta

        def _forward(x, edge_index, W_self1, W_neigh1, W_pool, b_pool, W_self2, W_neigh2, g1, beta1, g2, beta2):
            src, dst = (edge_index[0], edge_index[1])
            n = x.shape[0]
            deg = jax.ops.segment_sum(jnp.ones((src.shape[0],), x.dtype), dst, num_segments=n)
            agg_sum = jax.ops.segment_sum(x[src], dst, num_segments=n)
            h_mean = agg_sum / jnp.maximum(deg, 1.0)[:, None]
            out1 = x @ W_self1 + h_mean @ W_neigh1
            out1 = _batch_norm(out1, g1, beta1)
            hp = jax.nn.relu(x @ W_pool + b_pool)
            agg_max = jax.ops.segment_max(hp[src], dst, num_segments=n)
            h_max = jnp.where(deg[:, None] > 0, agg_max, 0.0)
            out2 = x @ W_self2 + h_max @ W_neigh2
            out2 = _batch_norm(out2, g2, beta2)
            return jax.nn.leaky_relu(out1 + out2, negative_slope=LEAKY_SLOPE)
        key = jax.random.key(seed)
        ks = jax.random.split(key, 9)
        x = jax.random.normal(ks[0], (N_NODES, D), dtype=jnp.float32)
        edge_index = jax.random.randint(ks[1], (2, N_EDGES), 0, N_NODES, dtype=jnp.int64)
        s = 0.05
        return {'x': x, 'edge_index': edge_index, 'W_self1': jax.random.normal(ks[2], (D, D), dtype=jnp.float32) * s, 'W_neigh1': jax.random.normal(ks[3], (D, D), dtype=jnp.float32) * s, 'W_pool': jax.random.normal(ks[4], (D, D), dtype=jnp.float32) * s, 'b_pool': jax.random.normal(ks[5], (D,), dtype=jnp.float32) * s, 'W_self2': jax.random.normal(ks[6], (D, D), dtype=jnp.float32) * s, 'W_neigh2': jax.random.normal(ks[7], (D, D), dtype=jnp.float32) * s, 'g1': jnp.ones((D,), jnp.float32), 'beta1': jnp.zeros((D,), jnp.float32), 'g2': jnp.ones((D,), jnp.float32), 'beta2': jnp.zeros((D,), jnp.float32)}
    _L1_gnn_all = _L1_gnn_setup()
    _L1_gnn_in = {k: v for k, v in _L1_gnn_all.items() if k in ('W_self1', 'W_neigh1', 'W_pool', 'b_pool', 'W_self2', 'W_neigh2', 'g1', 'beta1', 'g2', 'beta2')}
    del _L1_gnn_all
    return {'x': x, 'src': src, 'dst': dst, 'edge_attr_32': edge_attr_32, 'L0_gnn_mW1': _L0_gnn_in['mW1'], 'L0_gnn_mb1': _L0_gnn_in['mb1'], 'L0_gnn_mW2': _L0_gnn_in['mW2'], 'L0_gnn_mb2': _L0_gnn_in['mb2'], 'L0_gnn_gW1': _L0_gnn_in['gW1'], 'L0_gnn_gb1': _L0_gnn_in['gb1'], 'L0_gnn_gW2': _L0_gnn_in['gW2'], 'L0_gnn_gb2': _L0_gnn_in['gb2'], 'L0_gnn_uW1': _L0_gnn_in['uW1'], 'L0_gnn_ub1': _L0_gnn_in['ub1'], 'L0_gnn_uW2': _L0_gnn_in['uW2'], 'L0_gnn_ub2': _L0_gnn_in['ub2'], 'L0_gnn_ln_g': _L0_gnn_in['ln_g'], 'L0_gnn_ln_b': _L0_gnn_in['ln_b'], 'L1_gnn_W_self1': _L1_gnn_in['W_self1'], 'L1_gnn_W_neigh1': _L1_gnn_in['W_neigh1'], 'L1_gnn_W_pool': _L1_gnn_in['W_pool'], 'L1_gnn_b_pool': _L1_gnn_in['b_pool'], 'L1_gnn_W_self2': _L1_gnn_in['W_self2'], 'L1_gnn_W_neigh2': _L1_gnn_in['W_neigh2'], 'L1_gnn_g1': _L1_gnn_in['g1'], 'L1_gnn_beta1': _L1_gnn_in['beta1'], 'L1_gnn_g2': _L1_gnn_in['g2'], 'L1_gnn_beta2': _L1_gnn_in['beta2']}

def reference(x, src, dst, edge_attr_32, L0_gnn_mW1, L0_gnn_mb1, L0_gnn_mW2, L0_gnn_mb2, L0_gnn_gW1, L0_gnn_gb1, L0_gnn_gW2, L0_gnn_gb2, L0_gnn_uW1, L0_gnn_ub1, L0_gnn_uW2, L0_gnn_ub2, L0_gnn_ln_g, L0_gnn_ln_b, L1_gnn_W_self1, L1_gnn_W_neigh1, L1_gnn_W_pool, L1_gnn_b_pool, L1_gnn_W_self2, L1_gnn_W_neigh2, L1_gnn_g1, L1_gnn_beta1, L1_gnn_g2, L1_gnn_beta2):
    import jax
    import jax.numpy as jnp

    def _L0_gnn_ref(x, edge_index, edge_attr, mW1, mb1, mW2, mb2, gW1, gb1, gW2, gb2, uW1, ub1, uW2, ub2, ln_g, ln_b):
        import jax, jax.numpy as jnp
        import numpy as np
        N, E = (6250, 100000)
        ND, ED = (96, 32)

        def _gelu(x):
            return jax.nn.gelu(x, approximate=False)
        src, dst = (edge_index[0], edge_index[1])
        edge_input = jnp.concatenate([x[src], edge_attr], axis=-1)
        messages = _gelu(edge_input @ mW1 + mb1) @ mW2 + mb2
        gates = jax.nn.sigmoid(_gelu(edge_input @ gW1 + gb1) @ gW2 + gb2)
        aggregated = jax.ops.segment_sum(messages * gates, dst, num_segments=x.shape[0])
        combined = jnp.concatenate([x, aggregated], axis=-1)
        update = _gelu(combined @ uW1 + ub1) @ uW2 + ub2
        h = x + update
        mu = jnp.mean(h, axis=-1, keepdims=True)
        var = jnp.mean(jnp.square(h - mu), axis=-1, keepdims=True)
        return (h - mu) * jax.lax.rsqrt(var + 1e-05) * ln_g + ln_b

    def _L1_gnn_ref(x, edge_index, W_self1, W_neigh1, W_pool, b_pool, W_self2, W_neigh2, g1, beta1, g2, beta2):
        import jax, jax.numpy as jnp
        import numpy as np
        N_NODES = 12500
        N_EDGES = 100000
        D = 96
        BN_EPS = 1e-05
        LEAKY_SLOPE = 0.01

        def _batch_norm(h, gamma, beta):
            mu = h.mean(axis=0)
            var = jnp.mean(jnp.square(h - mu), axis=0)
            return gamma * (h - mu) * jax.lax.rsqrt(var + BN_EPS) + beta

        def _forward(x, edge_index, W_self1, W_neigh1, W_pool, b_pool, W_self2, W_neigh2, g1, beta1, g2, beta2):
            src, dst = (edge_index[0], edge_index[1])
            n = x.shape[0]
            deg = jax.ops.segment_sum(jnp.ones((src.shape[0],), x.dtype), dst, num_segments=n)
            agg_sum = jax.ops.segment_sum(x[src], dst, num_segments=n)
            h_mean = agg_sum / jnp.maximum(deg, 1.0)[:, None]
            out1 = x @ W_self1 + h_mean @ W_neigh1
            out1 = _batch_norm(out1, g1, beta1)
            hp = jax.nn.relu(x @ W_pool + b_pool)
            agg_max = jax.ops.segment_max(hp[src], dst, num_segments=n)
            h_max = jnp.where(deg[:, None] > 0, agg_max, 0.0)
            out2 = x @ W_self2 + h_max @ W_neigh2
            out2 = _batch_norm(out2, g2, beta2)
            return jax.nn.leaky_relu(out1 + out2, negative_slope=LEAKY_SLOPE)
        return _forward(x, edge_index, W_self1, W_neigh1, W_pool, b_pool, W_self2, W_neigh2, g1, beta1, g2, beta2)
    edge_index = jnp.stack([src, dst])
    h = jnp.maximum(_layernorm(x, axis=-1), 0.0)
    x = x + _L0_gnn_ref(h, edge_index, edge_attr_32, L0_gnn_mW1, L0_gnn_mb1, L0_gnn_mW2, L0_gnn_mb2, L0_gnn_gW1, L0_gnn_gb1, L0_gnn_gW2, L0_gnn_gb2, L0_gnn_uW1, L0_gnn_ub1, L0_gnn_uW2, L0_gnn_ub2, L0_gnn_ln_g, L0_gnn_ln_b)
    h = jnp.maximum(_layernorm(x, axis=-1), 0.0)
    x = x + _L1_gnn_ref(h, edge_index, L1_gnn_W_self1, L1_gnn_W_neigh1, L1_gnn_W_pool, L1_gnn_b_pool, L1_gnn_W_self2, L1_gnn_W_neigh2, L1_gnn_g1, L1_gnn_beta1, L1_gnn_g2, L1_gnn_beta2)
    return x

_drawn_inputs = setup_inputs


def setup_inputs(seed=0):
    import zlib

    import numpy as np

    out = dict(_drawn_inputs(seed))
    spreads = {'L0_gnn_mb1': (0.0, 0.301),
     'L0_gnn_mb2': (0.0, 0.1),
     'L0_gnn_gb1': (0.0, 2.0),
     'L0_gnn_ub1': (0.0, 0.281),
     'L0_gnn_ub2': (0.0, 0.1),
     'L0_gnn_ln_g': (1.0, 0.2),
     'L0_gnn_ln_b': (0.0, 0.1),
     'L1_gnn_g1': (1.0, 0.2),
     'L1_gnn_beta1': (0.0, 0.1),
     'L1_gnn_g2': (1.0, 0.2),
     'L1_gnn_beta2': (0.0, 0.1)}
    factors = {'L0_gnn_gW1': 7.775, 'L0_gnn_gW2': 8.0, 'L1_gnn_b_pool': 8.0}
    for name, (base, spread) in spreads.items():
        noise = np.random.default_rng([zlib.crc32(name.encode()), seed]).standard_normal(out[name].shape)
        drawn = base * np.exp(spread * noise) if base else spread * noise
        out[name] = jnp.asarray(drawn.astype(out[name].dtype))
    for name, factor in factors.items():
        out[name] = (out[name] * factor).astype(out[name].dtype)
    return out
```

```python
from contextlib import ExitStack

import concourse.bass as bass
from concourse import mybir

F32 = mybir.dt.float32
I32 = mybir.dt.int32
ALU = mybir.AluOpType
ACT = mybir.ActivationFunctionType

P = 128
N, E, D, DE = 6250, 106250, 96, 32
GROUP = 4
CHUNK = 4 * P
NCH = -(-N // CHUNK)
NPAD = NCH * CHUNK
NT = NPAD // P
LAST = N - (NCH - 1) * CHUNK
ET = -(-E // (P * GROUP)) * GROUP
EPAD = ET * P
NG = ET // GROUP
RING = 4
ROW0 = 2 * D
ROW1 = 2 * D + 1
BN_EPS = LN_EPS = 1e-5


class Step:

    def __init__(self, turn, slot, unroll, count):
        self.turn, self.slot, self.unroll, self.count = turn, slot, unroll, count

    def item(self, lag=0):
        slot, turn = self.slot - lag, self.turn
        while slot < 0:
            slot, turn = slot + self.unroll, turn - 1
        at = turn * self.unroll + slot
        if isinstance(at, int) and not 0 <= at < self.count:
            return None
        return at, slot, turn


def walk(engine, count, lags, unroll, peeled, body):
    for s in range(peeled):
        body(Step(s // unroll, s % unroll, unroll, count))
    with engine.Fori(peeled // unroll, count // unroll) as turn:
        for k in range(unroll):
            body(Step(turn, k, unroll, count))
    for s in range(count // unroll * unroll, count + lags):
        body(Step(s // unroll, s % unroll, unroll, count))


def walk_edges(engine, lags, body):
    walk(engine, NG, lags, RING, 2 * RING, body)


def walk_nodes(engine, lags, body):
    walk(engine, NCH, lags, 2, 6, body)


def wait(engine, sem, value):
    if not isinstance(value, int) or value > 0:
        engine.wait_ge(sem, value)


def hold(engine, passed):
    engine.sem_inc(passed, 1)


def gnn(nc, x, src_lanes, dst_lanes, dst_next_lanes, dst_ext, edge_attr_t,
        mW1, mb1, mW2, mb2, gW1, gb1, gW2, gb2, uW1, ub1, uW2, ub2, ln_g, ln_b,
        W_self1, W_neigh1, W_pool, b_pool, W_self2, W_neigh2, g1, beta1, g2, beta2, out):
    with ExitStack() as ctx:
        def sb(name, shape, dt=F32):
            return ctx.enter_context(nc.sbuf_tensor(name, shape, dt))

        def sem(name):
            return ctx.enter_context(nc.semaphore(name))

        def sems(name, n):
            return [sem(f"{name}{i}") for i in range(n)]

        table0 = nc.dram_tensor("table0", (NPAD, ROW0), F32)
        table1 = nc.dram_tensor("table1", (NPAD, ROW1), F32)
        same_dst = nc.dram_tensor("same_dst", (EPAD,), F32)

        x_nodes = sb("x_nodes", [P, NT, D])
        h_nodes = sb("h_nodes", [P, NT, D])
        h_feat = sb("h_feat", [D + 1, NPAD])
        sum_feat = sb("sum_feat", [D + 1, NPAD])
        max_feat = sb("max_feat", [D, NPAD])

        rows = sb("rows", [P, RING, GROUP * ROW1])
        indices = sb("indices", [P, RING, GROUP], I32)
        stream = sb("stream", [D, RING, GROUP * P])
        pre = sb("pre", [P, 2, GROUP * ROW0])
        gate_act = sb("gate_act", [P, 2, GROUP, D])
        msg = sb("msg", [P, 2, GROUP, D + 1])
        logit = sb("logit", [P, 2, GROUP])
        tanh = sb("tanh", [P, 2, GROUP])
        gate = sb("gate", [P, 2, GROUP])
        onehot = sb("onehot", [P, 2, GROUP, P])
        scanned = sb("scanned", [D, 2, GROUP * P])
        ends = sb("ends", [P, 2, GROUP, D])

        h_tile = sb("h_tile", [P, 2, 4, D])
        h_chunk = sb("h_chunk", [D + 1, 2, CHUNK])
        u_chunk = sb("u_chunk", [D + 1, 2, CHUNK])
        y_tile = sb("y_tile", [P, 2, 4, D])
        out_rows = sb("out_rows", [P, 2, 4 * ROW1])
        mean_chunk, shifted, y_chunk = u_chunk, scanned, h_chunk
        stats = sb("stats", [P, 2, 4, 6])
        mv = sb("mv", [P, 2, 4, 2])
        rstd = sb("rstd", [P, 2, 4])
        nmr = sb("nmr", [P, 2, 4])
        var_eps = sb("var_eps", [P, 4])
        var_eps2 = sb("var_eps2", [P, 4])
        power = sb("power", [P, 4])
        degree = sb("degree", [D + 1, 2, CHUNK])

        dst_i = sb("dst_i", [P, ET], I32)
        dst_rel = sb("dst_rel", [P, ET])
        is_end = sb("is_end", [P, ET])

        ident = sb("ident", [P, P])
        columns = sb("columns", [P, P])
        lane = sb("lane", [P, 1])
        ones = sb("ones", [P, P])
        w_table0 = sb("w_table0", [D + 1, ROW0])
        w_edge = sb("w_edge", [DE, ROW0])
        w_gate = sb("w_gate", [P, D])
        b_gate = sb("b_gate", [P, 1])
        w_m2 = sb("w_m2", [D, D])
        w_m2t = sb("w_m2t", [D, D + 1])
        w_u1_agg = sb("w_u1_agg", [D, D])
        w_u1_h = sb("w_u1_h", [D + 1, D])
        w_u1_sum = sb("w_u1_sum", [D + 1, D])
        w_u2 = sb("w_u2", [D + 1, D])
        scale_ln = sb("scale_ln", [P, D])
        shift_ln = sb("shift_ln", [P, D])
        w_pool = sb("w_pool", [D + 1, D])
        w_self = sb("w_self", [D, 2, D])
        w_neigh = sb("w_neigh", [D, 2, D])
        bn_scale = sb("bn_scale", [D, 2])
        bn_shift = sb("bn_shift", [D, 2])
        bn_stats = sb("bn_stats", [D, 2, NCH, 6])
        bn_mv = sb("bn_mv", [D, 2, 2])
        bn_rstd = sb("bn_rstd", [D, 2])
        bn_a = sb("bn_a", [D, 2])
        bn_am = sb("bn_am", [D, 2])
        bn_c = sb("bn_c", [D, 3])

        ps = ctx.enter_context(nc.psum_tensor("ps", [P, 8, 512], F32))

        edges_loaded = sem("edges_loaded")
        pool_passed = sem("pool_passed")
        dve_passed = sem("dve_passed")
        weights_loaded = sem("weights_loaded")
        x_loaded = sem("x_loaded")
        consts_made = sem("consts_made")
        columns_made = sem("columns_made")
        cleared = sem("cleared")
        same_made = sem("same_made")
        same_stored = sem("same_stored")
        dst_float = sem("dst_float")
        base_spread = sem("base_spread")
        dst_ready = sem("dst_ready")
        sums_zero = sem("sums_zero")
        m2_turned = sem("m2_turned")
        m2_copied = sem("m2_copied")
        u1_product = sem("u1_product")
        u1_ready = sem("u1_ready")
        a_bn = sem("a_bn")
        a_stats = sem("a_stats")
        a_eps = sem("a_eps")
        a_rstd = sem("a_rstd")
        a_nmr = sem("a_nmr")
        a_h = sem("a_h")
        a_turned = sem("a_turned")
        a_copied = sem("a_copied")
        a_kept = sem("a_kept")
        a_product = sem("a_product")
        a_evac = sem("a_evac")
        a_stored = sems("a_stored", 2)
        attr_loaded = sems("attr_loaded", RING)
        index_loaded = sems("index_loaded", RING)
        gathered = sems("gathered", RING)
        pre_product = sem("pre_product")
        pre_added = sem("pre_added")
        gate_gelu = sem("gate_gelu")
        msg_gelu = sem("msg_gelu")
        logits_done = sem("logits_done")
        tanh_done = sem("tanh_done")
        gate_done = sem("gate_done")
        onehot_done = sem("onehot_done")
        summed = sem("summed")
        window_added = sem("window_added")
        c_u = sem("c_u")
        c_gelu = sem("c_gelu")
        c_update = sem("c_update")
        c_hs = sem("c_hs")
        c_bn = sem("c_bn")
        c_stats = sem("c_stats")
        c_eps = sem("c_eps")
        c_rstd = sem("c_rstd")
        c_ln = sem("c_ln")
        c_bn2 = sem("c_bn2")
        c_stats2 = sem("c_stats2")
        c_eps2 = sem("c_eps2")
        c_rstd2 = sem("c_rstd2")
        c_nmr = sem("c_nmr")
        c_h = sem("c_h")
        c_turned = sem("c_turned")
        c_copied = sem("c_copied")
        c_kept = sem("c_kept")
        c_pool = sem("c_pool")
        c_evac = sem("c_evac")
        c_stored = sems("c_stored", 2)
        mask_loaded = sems("mask_loaded", RING)
        index1_loaded = sems("index1_loaded", RING)
        gathered1 = sems("gathered1", RING)
        sums_cleared = sem("sums_cleared")
        turned = sem("turned")
        scan_done = sem("scan_done")
        onehot1_done = sem("onehot1_done")
        turned_back = sem("turned_back")
        ends_done = sem("ends_done")
        picked = sem("picked")
        window1_added = sem("window1_added")
        e_degree = sem("e_degree")
        e_recip = sem("e_recip")
        e_spread = sem("e_spread")
        e_mean = sem("e_mean")
        e_out = sem("e_out")
        e_stats = sem("e_stats")
        e_kept = sem("e_kept")
        e_bn = sem("e_bn")
        e_pow = sem("e_pow")
        f_shift = sem("f_shift")
        f_sum = sem("f_sum")
        f_leaky = sem("f_leaky")
        f_turned = sem("f_turned")
        f_added = sem("f_added")
        f_stored = sems("f_stored", 2)

        block = ctx.enter_context(nc.Block())

        staging = rows[:, :, :].rearrange("p a b -> p (a b)").bitcast(I32)
        row_dst = staging[:, 0:ET]
        row_prev = staging[:, ET:2 * ET]
        next_i = staging[:, 2 * ET:3 * ET]
        same = onehot[:, :, :, :].rearrange("p a b c -> p (a b c)")[:, 0:ET]
        N_EDGE_LOADS, N_WEIGHT_LOADS = 4, 27

        def rows0(slot):
            return rows[:, slot, 0:GROUP * ROW0]

        def tile_rows(t):
            return t.rearrange("(t p) f -> p t f", p=P)

        @block.sync
        def _(sp):
            sp.dma_start(dst_i[:, :], dst_lanes).then_inc(edges_loaded, 16)
            sp.dma_start(row_dst, dst_ext[1:EPAD + 1].rearrange("(p t) -> p t", p=P)).then_inc(edges_loaded, 16)
            sp.dma_start(row_prev, dst_ext[0:EPAD].rearrange("(p t) -> p t", p=P)).then_inc(edges_loaded, 16)
            sp.dma_start(next_i, dst_next_lanes).then_inc(edges_loaded, 16)
            sp.dma_start(x_nodes[:, :, :], x).then_inc(x_loaded, 16)

            sp.wait_ge(same_made, 1)
            sp.dma_start(same_dst.rearrange("(p t) -> p t", p=P), same).then_inc(same_stored, 16)

            def store0(step):
                if (c := step.item(3)):
                    at, slot, turn = c
                    wait(sp, a_evac, at + 1)
                    sp.dma_start(tile_rows(table0)[:, bass.ds(at * 4, 4), :],
                                 pre[:, slot, :].rearrange("p (t f) -> p t f", f=ROW0)).then_inc(a_stored[slot], 16)
            walk_nodes(sp, 3, store0)

            def load0(step):
                at, slot, turn = step.item()
                wait(sp, pre_product, at - RING + 1)
                sp.dma_start(stream[0:DE, slot, :], edge_attr_t[:, bass.ds(at * CHUNK, CHUNK)])\
                  .then_inc(attr_loaded[slot], 16)
                wait(sp, gathered[slot], turn * 64)
                sp.dma_start(indices[:, slot, :], src_lanes[:, bass.ds(at * GROUP, GROUP)])\
                  .then_inc(index_loaded[slot], 16)
            walk_edges(sp, 0, load0)

            def store1(step):
                if (c := step.item(4)):
                    at, slot, turn = c
                    wait(sp, c_evac, at + 1)
                    sp.dma_start(tile_rows(table1)[:, bass.ds(at * 4, 4), :],
                                 out_rows[:, slot, :].rearrange("p (t f) -> p t f", f=ROW1))\
                      .then_inc(c_stored[slot], 16)
            walk_nodes(sp, 4, store1)

            sp.wait_ge(same_stored, 16)
            sp.wait_ge(pre_product, NG)
            for slot in range(RING):
                sp.wait_ge(gathered[slot], 64 * (NG // RING))

            def load1(step):
                at, slot, turn = step.item()
                wait(sp, scan_done, at - RING + 1)
                sp.dma_start(stream[:, slot, :],
                             same_dst[bass.ds(at * CHUNK, CHUNK)].partition_broadcast(D))\
                  .then_inc(mask_loaded[slot], 16)
                wait(sp, gathered1[slot], turn * 64)
                sp.dma_start(indices[:, slot, :], src_lanes[:, bass.ds(at * GROUP, GROUP)])\
                  .then_inc(index1_loaded[slot], 16)
            walk_edges(sp, 0, load1)

            def store_out(step):
                if (c := step.item(3)):
                    at, slot, turn = c
                    wait(sp, f_added, at + 1)
                    sp.dma_start(out[:, bass.ds(at * 4, 4), :], y_tile[:, slot, :, :]).then_inc(f_stored[slot], 16)
            walk_nodes(sp, 3, store_out)
            sp.wait_ge(f_stored[0], 16 * ((NCH + 1) // 2))
            sp.wait_ge(f_stored[1], 16 * (NCH // 2))



        @block.gpsimd
        def _(pool):
            nc.gpsimd.memset(power[:, :], -0.5).then_inc(consts_made, 1)
            nc.gpsimd.memset(ident[:, :], 0.0).then_inc(consts_made, 1)
            nc.gpsimd.memset(ones[:, :], 1.0).then_inc(consts_made, 1)
            pool.wait_ge(consts_made, 3)
            nc.gpsimd.affine_select(out=ident[:, :], in_=ident[:, :], compare_op=ALU.not_equal, fill=1.0,
                                    base=0, pattern=[[-1, P]], channel_multiplier=1).then_inc(consts_made, 1)
            nc.gpsimd.iota(columns[:, :], [[1, P]], 0, 0, allow_small_or_imprecise_dtypes=True)\
              .then_inc(columns_made, 1)
            nc.gpsimd.iota(lane[:, :], [[0, 1]], 0, 1, allow_small_or_imprecise_dtypes=True)\
              .then_inc(columns_made, 1)
            pool.wait_ge(columns_made, 2)
            nc.gpsimd.memset(h_chunk[D:D + 1, :, :], 1.0).then_inc(cleared, 1)
            nc.gpsimd.memset(h_feat[D:D + 1, :], 1.0).then_inc(cleared, 1)
            nc.gpsimd.memset(u_chunk[D:D + 1, :, :], 1.0).then_inc(cleared, 1)
            pool.wait_ge(cleared, 3)
            nc.gpsimd.memset(max_feat[:, :], 0.0).then_inc(cleared, 1)
            pool.wait_ge(cleared, 4)
            for j in range(GROUP):
                nc.gpsimd.memset(out_rows[:, :, j * ROW1 + D:j * ROW1 + D + 1], 1.0).then_inc(cleared, 1)

            def prepare(step):
                if (c := step.item(0)):
                    at, slot, turn = c
                    wait(pool, a_stats, at + 1)
                    wait(pool, a_rstd, at)
                    hold(pool, pool_passed)
                    nc.gpsimd.tensor_scalar(var_eps[:, :], mv[:, slot, :, 1], LN_EPS, None, ALU.add)\
                      .then_inc(a_eps, 1)
                    wait(pool, a_eps, at + 1)
                    wait(pool, a_nmr, at - 1)
                    wait(pool, a_h, at - 1)
                    nc.gpsimd.tensor_tensor(rstd[:, slot, :], var_eps[:, :], power[:, :], ALU.pow)\
                      .then_inc(a_rstd, 1)
                if (c := step.item(2)):
                    at, slot, turn = c
                    wait(pool, a_h, at + 1)
                    nc.gpsimd.tensor_copy(h_nodes[:, bass.ds(at * 4, 4), :], h_tile[:, slot, :, :]).then_inc(a_kept, 1)
                    wait(pool, a_copied, at + 1)
                    nc.gpsimd.tensor_copy(h_feat[0:D, bass.ds(at * CHUNK, CHUNK)], h_chunk[0:D, slot, :])\
                      .then_inc(a_kept, 1)
            walk_nodes(pool, 2, prepare)

            pool.wait_ge(a_stored[0], 16 * ((NCH + 1) // 2))
            pool.wait_ge(a_stored[1], 16 * (NCH // 2))
            pool.wait_ge(dst_ready, 3)

            def gather0(step):
                at, slot, turn = step.item()
                wait(pool, index_loaded[slot], (turn + 1) * 16)
                wait(pool, pre_added, at - RING + 1)
                hold(pool, pool_passed)
                for j in range(GROUP):
                    nc.gpsimd.indirect_dma_start(
                        rows[:, slot, j * ROW0:(j + 1) * ROW0], None, table0[:, :],
                        bass.IndirectOffsetOnAxis(ap=indices[:, slot, j:j + 1], axis=0)).then_inc(gathered[slot], 16)
            walk_edges(pool, 0, gather0)

            def update(step):
                if (c := step.item(1)):
                    at, slot, turn = c
                    wait(pool, c_stats, at + 1)
                    wait(pool, c_rstd, at)
                    hold(pool, pool_passed)
                    nc.gpsimd.tensor_scalar(var_eps[:, :], mv[:, slot, :, 1], LN_EPS, None, ALU.add)\
                      .then_inc(c_eps, 1)
                    wait(pool, c_eps, at + 1)
                    wait(pool, c_h, at - 1)
                    nc.gpsimd.tensor_tensor(rstd[:, slot, :], var_eps[:, :], power[:, :], ALU.pow)\
                      .then_inc(c_rstd, 1)
                if (c := step.item(2)):
                    at, slot, turn = c
                    wait(pool, c_stats2, at + 1)
                    wait(pool, c_rstd2, at)
                    hold(pool, pool_passed)
                    nc.gpsimd.tensor_scalar(var_eps2[:, :], mv[:, slot, :, 1], LN_EPS, None, ALU.add)\
                      .then_inc(c_eps2, 1)
                    wait(pool, c_eps2, at + 1)
                    nc.gpsimd.tensor_tensor(rstd[:, slot, :], var_eps2[:, :], power[:, :], ALU.pow)\
                      .then_inc(c_rstd2, 1)
                if (c := step.item(4)):
                    at, slot, turn = c
                    wait(pool, c_copied, at + 1)
                    nc.gpsimd.tensor_copy(h_feat[0:D, bass.ds(at * CHUNK, CHUNK)], h_chunk[0:D, slot, :])\
                      .then_inc(c_kept, 1)
            walk_nodes(pool, 4, update)

            pool.wait_ge(c_stored[0], 16 * ((NCH + 1) // 2))
            pool.wait_ge(c_stored[1], 16 * (NCH // 2))

            def gather1(step):
                at, slot, turn = step.item()
                wait(pool, index1_loaded[slot], (turn + 1) * 16)
                wait(pool, picked, at - RING + 1)
                hold(pool, pool_passed)
                for j in range(GROUP):
                    nc.gpsimd.indirect_dma_start(
                        rows[:, slot, j * ROW1:(j + 1) * ROW1], None, table1[:, :],
                        bass.IndirectOffsetOnAxis(ap=indices[:, slot, j:j + 1], axis=0)).then_inc(gathered1[slot], 16)
            walk_edges(pool, 0, gather1)

            pool.wait_ge(e_bn, 2)
            nc.gpsimd.tensor_scalar(bn_c[:, 0:2], bn_mv[:, :, 1], BN_EPS, None, ALU.add).then_inc(e_pow, 1)
            pool.wait_ge(e_pow, 1)
            nc.gpsimd.tensor_tensor(bn_rstd[:, :], bn_c[:, 0:2], power[0:D, 0:2], ALU.pow).then_inc(e_pow, 1)

        @block.scalar
        def _(act):
            def load(to, of):
                act.dma_start(to, of).then_inc(weights_loaded, 16)

            def row(v):
                return v.rearrange("(a n) -> a n", a=1)

            def col(v):
                return v.rearrange("(n a) -> n a", a=1)

            load(w_table0[0:D, 0:D], mW1[0:D, :])
            load(w_table0[0:D, D:ROW0], gW1[0:D, :])
            load(w_table0[D:D + 1, 0:D], row(mb1))
            load(w_table0[D:D + 1, D:ROW0], row(gb1))
            load(w_edge[:, 0:D], mW1[D:D + DE, :])
            load(w_edge[:, D:ROW0], gW1[D:D + DE, :])
            load(w_gate[:, :], gW2.rearrange("n a -> (n a)").partition_broadcast(P))
            load(b_gate[:, :], gb2.partition_broadcast(P))
            load(w_m2[:, :], mW2)
            load(w_m2t[:, D:D + 1], col(mb2))
            load(w_u1_h[0:D, :], uW1[0:D, :])
            load(w_u1_h[D:D + 1, :], row(ub1))
            load(w_u1_agg[:, :], uW1[D:2 * D, :])
            load(w_u2[0:D, :], uW2)
            load(w_u2[D:D + 1, :], row(ub2))
            load(scale_ln[:, :], ln_g.partition_broadcast(P))
            load(shift_ln[:, :], ln_b.partition_broadcast(P))
            load(w_pool[0:D, :], W_pool)
            load(w_pool[D:D + 1, :], row(b_pool))
            for k, (s, n, g, b) in enumerate(((W_self1, W_neigh1, g1, beta1), (W_self2, W_neigh2, g2, beta2))):
                load(w_self[:, k, :], s)
                load(w_neigh[:, k, :], n)
                load(bn_scale[:, k:k + 1], col(g))
            act.dma_start(bn_shift[:, 0:1], col(beta1)).then_inc(weights_loaded, 16)
            act.dma_start(bn_shift[:, 1:2], col(beta2)).then_inc(weights_loaded, 16)

            def prepare(step):
                if (c := step.item(1)):
                    at, slot, turn = c
                    wait(act, a_nmr, at + 1)
                    wait(act, a_turned, at - 1)
                    wait(act, a_kept, 2 * (at - 1))
                    for j in range(4):
                        last = nc.scalar.activation(h_tile[:, slot, j, :], x_nodes[:, bass.ds(at * 4 + j, 1), :]
                                                    .rearrange("p a f -> p (a f)"), ACT.Relu,
                                                    bias=nmr[:, slot, j:j + 1], scale=rstd[:, slot, j:j + 1])
                    last.then_inc(a_h, 1)
                if (c := step.item(3)):
                    at, slot, turn = c
                    wait(act, a_product, at + 1)
                    wait(act, a_stored[slot], turn * 16)
                    nc.scalar.activation(pre[:, slot, :].rearrange("p (b f) -> p b f", b=2),
                                         ps[:, 2 + 2 * slot:4 + 2 * slot, 0:2 * ROW0], ACT.Copy).then_inc(a_evac, 1)
            walk_nodes(act, 3, prepare)

            act.wait_ge(a_stored[0], 16 * ((NCH + 1) // 2))
            act.wait_ge(a_stored[1], 16 * (NCH // 2))

            def edges0(step):
                if (c := step.item(1)):
                    at, slot, turn = c
                    wait(act, logits_done, at + 1)
                    wait(act, gate_done, at - 1)
                    nc.scalar.activation(tanh[:, slot % 2, :], logit[:, slot % 2, :], ACT.Tanh,
                                         bias=b_gate[:, 0:1], scale=0.5).then_inc(tanh_done, 1)
                if (c := step.item(0)):
                    at, slot, turn = c
                    z = pre[:, slot % 2, :].rearrange("p (t k f) -> p t k f", t=GROUP, k=2)
                    wait(act, pre_added, at + 1)
                    wait(act, logits_done, at - 1)
                    nc.scalar.activation(gate_act[:, slot % 2, :, :], z[:, :, 1, :], ACT.Gelu).then_inc(gate_gelu, 1)
                    wait(act, summed, at - 1)
                    nc.scalar.activation(msg[:, slot % 2, :, 0:D], z[:, :, 0, :], ACT.Gelu).then_inc(msg_gelu, 1)
            act.wait_ge(u1_ready, 1)
            walk_edges(act, 1, edges0)

            act.wait_ge(cleared, 8)

            def update(step):
                if (c := step.item(3)):
                    at, slot, turn = c
                    wait(act, c_nmr, at + 1)
                    wait(act, c_stored[slot], turn * 16)
                    for j in range(4):
                        last = nc.scalar.activation(out_rows[:, slot, j * ROW1:j * ROW1 + D],
                                                    x_nodes[:, bass.ds(at * 4 + j, 1), :]
                                                    .rearrange("p a f -> p (a f)"), ACT.Relu,
                                                    bias=nmr[:, slot, j:j + 1], scale=rstd[:, slot, j:j + 1])
                    last.then_inc(c_h, 1)
                if (c := step.item(0)):
                    at, slot, turn = c
                    wait(act, c_u, at + 1)
                    wait(act, c_update, at - 1)
                    nc.scalar.activation(u_chunk[0:D, slot, :], ps[0:D, slot, :], ACT.Gelu).then_inc(c_gelu, 1)
                if (c := step.item(4)):
                    at, slot, turn = c
                    wait(act, c_pool, at + 1)
                    nc.scalar.activation(out_rows[:, slot, :].rearrange("p (t f) -> p t f", f=ROW1)[:, :, D + 1:ROW1],
                                         ps[:, 6 + slot, 0:4 * D].rearrange("p (t f) -> p t f", f=D), ACT.Relu)\
                      .then_inc(c_evac, 1)
            walk_nodes(act, 4, update)

            def edges1(step):
                if (c := step.item(1)):
                    at, slot, turn = c
                    wait(act, turned_back, at + 1)
                    wait(act, picked, at - 1)
                    for j in range(GROUP):
                        last = nc.scalar.activation(ends[:, slot % 2, j, :], ps[:, 2 + slot % 2, j * D:(j + 1) * D],
                                                    ACT.Copy, scale=is_end[:, bass.ds(at * GROUP + j, 1)])
                    last.then_inc(ends_done, 1)
            walk_edges(act, 1, edges1)

            def outs(step):
                if (c := step.item(2)):
                    at, slot, turn = c
                    wait(act, e_out, at + 1)
                    nc.scalar.activation(sum_feat[0:D, bass.ds(at * CHUNK, CHUNK)], ps[0:D, 2 + slot, :], ACT.Copy)
                    nc.scalar.activation(max_feat[:, bass.ds(at * CHUNK, CHUNK)], ps[0:D, 4 + slot, :], ACT.Copy)\
                      .then_inc(e_kept, 1)
            walk_nodes(act, 2, outs)

            act.wait_ge(e_bn, 8)

            def finish(step):
                if (c := step.item(0)):
                    at, slot, turn = c
                    wait(act, f_leaky, at - 1)
                    nc.scalar.activation(shifted[:, slot, :], sum_feat[0:D, bass.ds(at * CHUNK, CHUNK)], ACT.Identity,
                                         bias=bn_c[:, 2:3], scale=bn_a[:, 0:1]).then_inc(f_shift, 1)
            walk_nodes(act, 0, finish)

        @block.tensor
        def _(pe):
            pe.wait_ge(consts_made, 4)
            pe.wait_ge(dst_float, 1)
            half = ET // 2
            for k in range(2):
                last = nc.tensor.matmul(ps[:, 6 + k, 0:half], ones[0:1, :], dst_rel[0:1, k * half:(k + 1) * half],
                                        start=True, stop=True)
            last.then_inc(base_spread, 1)

            pe.wait_ge(weights_loaded, 16 * N_WEIGHT_LOADS)
            pe.wait_ge(cleared, 1)

            def prepare(step):
                if (c := step.item(1)):
                    at, slot, turn = c
                    wait(pe, a_h, at + 1)
                    wait(pe, a_copied, at - 1)
                    for j in range(4):
                        last = nc.tensor.transpose(ps[0:D, slot, j * P:(j + 1) * P], h_tile[:, slot, j, :], ident[:, :])
                    last.then_inc(a_turned, 1)
                if (c := step.item(2)):
                    at, slot, turn = c
                    wait(pe, a_copied, at + 1)
                    wait(pe, a_evac, at - 1)
                    for j in range(4):
                        last = nc.tensor.matmul(ps[:, 2 + 2 * slot + j // 2, (j % 2) * ROW0:(j % 2 + 1) * ROW0],
                                                h_chunk[:, slot, j * P:(j + 1) * P], w_table0[:, :],
                                                start=True, stop=True)
                    last.then_inc(a_product, 1)
            walk_nodes(pe, 2, prepare)

            pe.wait_ge(dst_ready, 3)
            nc.tensor.transpose(ps[0:D, 6, 0:D], w_m2[:, :], ident[0:D, 0:D]).then_inc(m2_turned, 1)
            pe.wait_ge(m2_copied, 1)
            nc.tensor.matmul(ps[0:D + 1, 7, 0:D], w_m2t[:, :], w_u1_agg[:, :], start=True, stop=True)\
              .then_inc(u1_product, 1)

            pe.wait_ge(a_evac, NCH)
            pe.wait_ge(a_copied, NCH)

            def edges0(step):
                if (c := step.item(0)):
                    at, slot, turn = c
                    wait(pe, attr_loaded[slot], (turn + 1) * 16)
                    wait(pe, pre_added, at - 1)
                    for j in range(GROUP):
                        last = nc.tensor.matmul(
                            ps[:, 2 * (slot % 2) + j // 2, (j % 2) * ROW0:(j % 2 + 1) * ROW0],
                            stream[0:DE, slot, j * P:(j + 1) * P], w_edge[:, :], start=True, stop=True)
                    last.then_inc(pre_product, 1)
                if (c := step.item(1)):
                    at, slot, turn = c
                    wait(pe, msg_gelu, at + 1)
                    wait(pe, onehot_done, at + 1)
                    wait(pe, window_added, 4 * (at - 1))
                    for j in range(GROUP):
                        last = nc.tensor.matmul(ps[0:D + 1, 4 + slot % 2, j * P:(j + 1) * P], msg[:, slot % 2, j, :],
                                                onehot[:, slot % 2, j, :], start=True, stop=True)
                    last.then_inc(summed, 1)
            walk_edges(pe, 1, edges0)

            pe.wait_ge(window_added, ET)
            pe.wait_ge(u1_ready, 2)
            pe.wait_ge(a_kept, 2 * NCH)
            pe.wait_ge(cleared, 8)

            def update(step):
                if (c := step.item(0)):
                    at, slot, turn = c
                    wait(pe, c_gelu, at - 1)
                    nc.tensor.matmul(ps[0:D, slot, :], w_u1_h[:, :], h_feat[:, bass.ds(at * CHUNK, CHUNK)],
                                     start=True, stop=False)
                    nc.tensor.matmul(ps[0:D, slot, :], w_u1_sum[:, :], sum_feat[:, bass.ds(at * CHUNK, CHUNK)],
                                     start=False, stop=True).then_inc(c_u, 1)
                if (c := step.item(1)):
                    at, slot, turn = c
                    wait(pe, c_gelu, at + 1)
                    wait(pe, c_hs, at - 1)
                    for j in range(4):
                        last = nc.tensor.matmul(ps[:, 2 + slot, j * D:(j + 1) * D], u_chunk[:, slot, j * P:(j + 1) * P],
                                                w_u2[:, :], start=True, stop=True)
                    last.then_inc(c_update, 1)
                if (c := step.item(3)):
                    at, slot, turn = c
                    wait(pe, c_h, at + 1)
                    wait(pe, c_copied, at - 1)
                    for j in range(4):
                        last = nc.tensor.transpose(ps[0:D, 4 + slot, j * P:(j + 1) * P],
                                                   out_rows[:, slot, j * ROW1:j * ROW1 + D], ident[:, :])
                    last.then_inc(c_turned, 1)
                if (c := step.item(4)):
                    at, slot, turn = c
                    wait(pe, c_copied, at + 1)
                    wait(pe, c_evac, at - 1)
                    for j in range(4):
                        last = nc.tensor.matmul(ps[:, 6 + slot, j * D:(j + 1) * D], h_chunk[:, slot, j * P:(j + 1) * P],
                                                w_pool[:, :], start=True, stop=True)
                    last.then_inc(c_pool, 1)
            walk_nodes(pe, 4, update)

            pe.wait_ge(c_evac, NCH)
            pe.wait_ge(c_copied, NCH)
            pe.wait_ge(c_hs, NCH)

            def edges1(step):
                if (c := step.item(0)):
                    at, slot, turn = c
                    wait(pe, gathered1[slot], (turn + 1) * 64)
                    wait(pe, scan_done, at - 1)
                    for j in range(GROUP):
                        last = nc.tensor.transpose(ps[0:D, slot % 2, j * P:(j + 1) * P],
                                                   rows[:, slot, j * ROW1 + D + 1:(j + 1) * ROW1], ident[:, :])
                    last.then_inc(turned, 1)
                if (c := step.item(1)):
                    at, slot, turn = c
                    wait(pe, scan_done, at + 1)
                    wait(pe, ends_done, at - 1)
                    for j in range(GROUP):
                        last = nc.tensor.transpose(ps[:, 2 + slot % 2, j * D:(j + 1) * D],
                                                   scanned[:, slot % 2, j * P:(j + 1) * P], ident[0:D, 0:D])
                    last.then_inc(turned_back, 1)
                if (c := step.item(2)):
                    at, slot, turn = c
                    wait(pe, ends_done, at + 1)
                    wait(pe, onehot1_done, at + 1)
                    wait(pe, window1_added, 8 * (at - 1))
                    for j in range(GROUP):
                        nc.tensor.matmul(ps[0:D + 1, 4 + slot % 2, j * P:(j + 1) * P],
                                         rows[:, slot, j * ROW1:j * ROW1 + D + 1],
                                         onehot[:, slot % 2, j, :], start=True, stop=True)
                        last = nc.tensor.matmul(ps[0:D, 6 + slot % 2, j * P:(j + 1) * P], ends[:, slot % 2, j, :],
                                                onehot[:, slot % 2, j, :], start=True, stop=True)
                    last.then_inc(picked, 1)
            walk_edges(pe, 2, edges1)

            pe.wait_ge(window1_added, 2 * ET)
            pe.wait_ge(c_kept, NCH)

            def outs(step):
                if (c := step.item(0)):
                    at, slot, turn = c
                    wait(pe, e_recip, at + 1)
                    wait(pe, e_mean, at - 1)
                    nc.tensor.matmul(ps[0:D, slot, :], ones[D:D + 1, 0:D], degree[D:D + 1, slot, :],
                                     start=True, stop=True).then_inc(e_spread, 1)
                if (c := step.item(1)):
                    at, slot, turn = c
                    wait(pe, e_mean, at + 1)
                    wait(pe, e_kept, at - 1)
                    for k, near in enumerate((mean_chunk[0:D, slot, :], max_feat[:, bass.ds(at * CHUNK, CHUNK)])):
                        nc.tensor.matmul(ps[0:D, 2 + 2 * k + slot, :], w_self[:, k, :],
                                         h_feat[0:D, bass.ds(at * CHUNK, CHUNK)], start=True, stop=False)
                        last = nc.tensor.matmul(ps[0:D, 2 + 2 * k + slot, :], w_neigh[:, k, :], near,
                                                start=False, stop=True)
                    last.then_inc(e_out, 1)
            walk_nodes(pe, 1, outs)

            def finish(step):
                if (c := step.item(2)):
                    at, slot, turn = c
                    wait(pe, f_leaky, at + 1)
                    wait(pe, f_added, at - 1)
                    for j in range(4):
                        last = nc.tensor.transpose(ps[:, 6 + slot, j * D:(j + 1) * D],
                                                   y_chunk[0:D, slot, j * P:(j + 1) * P], ident[0:D, 0:D])
                    last.then_inc(f_turned, 1)
            walk_nodes(pe, 2, finish)

        @block.vector
        def _(dve):
            dve.wait_ge(edges_loaded, 16 * N_EDGE_LOADS)
            nc.vector.tensor_copy(dst_rel[:, :], dst_i[:, :]).then_inc(dst_float, 1)
            nc.vector.tensor_tensor(same, row_dst, row_prev, ALU.is_equal).then_inc(same_made, 1)
            nc.vector.tensor_tensor(is_end[:, :], dst_i[:, :], next_i, ALU.not_equal).then_inc(dst_float, 1)
            dve.wait_ge(columns_made, 2)
            nc.vector.tensor_scalar(lane[:, :], lane[:, :], float(P - 1), None, ALU.is_ge).then_inc(dst_float, 1)
            dve.wait_ge(dst_float, 3)
            nc.vector.tensor_scalar(is_end[:, :], is_end[:, :], lane[:, 0:1], None, ALU.max).then_inc(dst_ready, 1)
            dve.wait_ge(base_spread, 1)
            half = ET // 2
            for k in range(2):
                nc.vector.tensor_tensor(dst_rel[:, k * half:(k + 1) * half], dst_rel[:, k * half:(k + 1) * half],
                                        ps[:, 6 + k, 0:half], ALU.subtract).then_inc(dst_ready, 1)
            nc.vector.memset(msg[:, :, :, D:D + 1], 1.0).then_inc(sums_zero, 1)
            nc.vector.memset(sum_feat[:, :], 0.0).then_inc(sums_zero, 1)

            def moments(of, slot, done, ready):
                hold(dve, dve_passed)
                for j in range(4):
                    nc.vector.bn_stats(stats[:, slot, j, :], of(j)).then_inc(done[0], 1)
                wait(dve, done[0], done[1])
                hold(dve, dve_passed)
                for j in range(4):
                    last = nc.vector.bn_aggr(mv[:, slot, j, :], stats[:, slot, j, :])
                last.then_inc(ready, 1)

            def minus_mean_rstd(slot, done):
                nc.vector.scalar_tensor_tensor(out=nmr[:, slot, :], in0=mv[:, slot, :, 0], scalar=-1.0,
                                               in1=rstd[:, slot, :], op0=ALU.mult, op1=ALU.mult).then_inc(done, 1)

            def node_tile(t, at, j):
                return t[:, bass.ds(at * 4 + j, 1), :].rearrange("p a f -> p (a f)")

            dve.wait_ge(x_loaded, 16)

            def prepare(step):
                if (c := step.item(0)):
                    at, slot, turn = c
                    wait(dve, a_nmr, at - 1)
                    moments(lambda j: node_tile(x_nodes, at, j), slot, (a_bn, 4 * at + 4), a_stats)
                if (c := step.item(1)):
                    at, slot, turn = c
                    wait(dve, a_rstd, at + 1)
                    wait(dve, a_h, at - 1)
                    minus_mean_rstd(slot, a_nmr)
                if (c := step.item(2)):
                    at, slot, turn = c
                    wait(dve, a_turned, at + 1)
                    wait(dve, a_product, at - 1)
                    wait(dve, a_kept, 2 * (at - 1))
                    nc.vector.tensor_copy(h_chunk[0:D, slot, :], ps[0:D, slot, :]).then_inc(a_copied, 1)
            walk_nodes(dve, 2, prepare)

            dve.wait_ge(weights_loaded, 16 * N_WEIGHT_LOADS)
            dve.wait_ge(m2_turned, 1)
            nc.vector.tensor_copy(w_m2t[:, 0:D], ps[0:D, 6, 0:D]).then_inc(m2_copied, 1)
            nc.vector.tensor_scalar(b_gate[:, :], b_gate[:, :], 0.5, None, ALU.mult).then_inc(u1_ready, 1)
            dve.wait_ge(u1_product, 1)
            nc.vector.tensor_copy(w_u1_sum[:, :], ps[0:D + 1, 7, 0:D]).then_inc(u1_ready, 1)
            dve.wait_ge(sums_zero, 2)
            dve.wait_ge(same_stored, 16)

            def bases(at):
                return nc.values_load_multi_w_load_instructions(
                    dst_i[0:1, bass.ds(at * GROUP, GROUP)], engines=[mybir.EngineType.DVE], min_val=0, max_val=N,
                    skip_runtime_bounds_check_because="destinations are node numbers, the padding's is N")[1]

            def edges0(step):
                if (c := step.item(1)):
                    at, slot, turn = c
                    wait(dve, gate_gelu, at + 1)
                    wait(dve, tanh_done, at - 1)
                    for j in range(GROUP):
                        last = nc.vector.tensor_tensor_reduce(
                            out=gate_act[:, slot % 2, j, :], in0=gate_act[:, slot % 2, j, :], in1=w_gate[:, :],
                            scale=1.0, scalar=0.0, op0=ALU.mult, op1=ALU.add, accum_out=logit[:, slot % 2, j:j + 1])
                    last.then_inc(logits_done, 1)
                if (c := step.item(0)):
                    at, slot, turn = c
                    wait(dve, gathered[slot], (turn + 1) * 64)
                    wait(dve, pre_product, at + 1)
                    wait(dve, msg_gelu, at - 1)
                    nc.vector.tensor_tensor(pre[:, slot % 2, :].rearrange("p (b f) -> p b f", b=2),
                                            rows0(slot).rearrange("p (b f) -> p b f", b=2),
                                            ps[:, 2 * (slot % 2):2 * (slot % 2) + 2, 0:2 * ROW0], ALU.add)\
                      .then_inc(pre_added, 1)
                one, two = step.item(1), step.item(2)
                if one:
                    at, slot, turn = one
                    wait(dve, tanh_done, at + 1)
                    wait(dve, summed, at - 1)
                    nc.vector.tensor_scalar(gate[:, slot % 2, :], tanh[:, slot % 2, :], 0.5, 0.5, ALU.mult, ALU.add)\
                      .then_inc(gate_done, 1)
                if two:
                    wait(dve, summed, two[0] + 1)
                    base = bases(two[0])
                if one:
                    wait(dve, gate_done, one[0] + 1)
                for j in range(GROUP):
                    if one:
                        at, slot, turn = one
                        last = nc.vector.tensor_scalar(onehot[:, slot % 2, j, :], columns[:, :],
                                                       dst_rel[:, bass.ds(at * GROUP + j, 1)],
                                                       gate[:, slot % 2, j:j + 1], ALU.is_equal, ALU.mult)
                        if j == GROUP - 1:
                            last.then_inc(onehot_done, 1)
                    if two:
                        at, slot, turn = two
                        window = sum_feat[:, bass.ds(base[j], P)]
                        wait(dve, window_added, at * GROUP + j)
                        nc.vector.tensor_tensor(window, window, ps[0:D + 1, 4 + slot % 2, j * P:(j + 1) * P], ALU.add)\
                          .then_inc(window_added, 1)
            walk_edges(dve, 2, edges0)

            def update(step):
                if (c := step.item(3)):
                    at, slot, turn = c
                    wait(dve, c_rstd2, at + 1)
                    wait(dve, c_h, at - 1)
                    minus_mean_rstd(slot, c_nmr)
                if (c := step.item(1)):
                    at, slot, turn = c
                    wait(dve, c_update, at + 1)
                    nc.vector.tensor_tensor(h_tile[:, slot, :, :], ps[:, 2 + slot, 0:4 * D]
                                            .rearrange("p (t f) -> p t f", f=D),
                                            h_nodes[:, bass.ds(at * 4, 4), :], ALU.add).then_inc(c_hs, 1)
                    wait(dve, c_hs, at + 1)
                    moments(lambda j: h_tile[:, slot, j, :], slot, (c_bn, 4 * at + 4), c_stats)
                if (c := step.item(2)):
                    at, slot, turn = c
                    wait(dve, c_rstd, at + 1)
                    for j in range(4):
                        last = nc.vector.tensor_scalar(y_tile[:, slot, j, :], h_tile[:, slot, j, :],
                                                       mv[:, slot, j, 0:1], rstd[:, slot, j:j + 1],
                                                       ALU.subtract, ALU.mult)
                    last.then_inc(c_ln, 1)
                    y, chunk = y_tile[:, slot, :, :], x_nodes[:, bass.ds(at * 4, 4), :]
                    wait(dve, c_ln, 4 * at + 1)
                    nc.vector.tensor_tensor(y, y, scale_ln[:, :].unsqueeze(1).to_broadcast([P, 4, D]), ALU.mult)\
                      .then_inc(c_ln, 1)
                    wait(dve, c_ln, 4 * at + 2)
                    nc.vector.tensor_tensor(y, y, shift_ln[:, :].unsqueeze(1).to_broadcast([P, 4, D]), ALU.add)\
                      .then_inc(c_ln, 1)
                    wait(dve, c_ln, 4 * at + 3)
                    nc.vector.tensor_tensor(chunk, chunk, y, ALU.add).then_inc(c_ln, 1)
                    wait(dve, c_ln, 4 * at + 4)
                    moments(lambda j: node_tile(x_nodes, at, j), slot, (c_bn2, 4 * at + 4), c_stats2)
                if (c := step.item(3)):
                    at, slot, turn = c
                    wait(dve, c_turned, at + 1)
                    wait(dve, c_pool, at - 1)
                    wait(dve, c_kept, at - 1)
                    nc.vector.tensor_copy(h_chunk[0:D, slot, :], ps[0:D, 4 + slot, :]).then_inc(c_copied, 1)
            dve.wait_ge(a_kept, 2 * NCH)
            walk_nodes(dve, 3, update)

            dve.wait_ge(c_u, NCH)
            nc.vector.memset(sum_feat[:, :], 0.0).then_inc(sums_cleared, 1)
            dve.wait_ge(sums_cleared, 1)

            def edges1(step):
                if (c := step.item(0)):
                    at, slot, turn = c
                    wait(dve, turned, at + 1)
                    wait(dve, mask_loaded[slot], (turn + 1) * 16)
                    wait(dve, turned_back, at - 1)
                    nc.vector.tensor_tensor_scan(scanned[:, slot % 2, :], stream[:, slot, :], ps[0:D, slot % 2, :],
                                                 0.0, ALU.mult, ALU.max).then_inc(scan_done, 1)
                one, three = step.item(1), step.item(3)
                if one:
                    wait(dve, picked, one[0] - 1)
                if three:
                    wait(dve, picked, three[0] + 1)
                    base = bases(three[0])
                for j in range(GROUP):
                    if one:
                        at, slot, turn = one
                        last = nc.vector.tensor_scalar(onehot[:, slot % 2, j, :], columns[:, :],
                                                       dst_rel[:, bass.ds(at * GROUP + j, 1)], None, ALU.is_equal)
                        if j == GROUP - 1:
                            last.then_inc(onehot1_done, 1)
                    if three:
                        at, slot, turn = three
                        window = sum_feat[:, bass.ds(base[j], P)]
                        wait(dve, window1_added, (at * GROUP + j) * 2)
                        nc.vector.tensor_tensor(window, window, ps[0:D + 1, 4 + slot % 2, j * P:(j + 1) * P], ALU.add)\
                          .then_inc(window1_added, 1)
                        window = max_feat[:, bass.ds(base[j], P)]
                        nc.vector.tensor_tensor(window, window, ps[0:D, 6 + slot % 2, j * P:(j + 1) * P], ALU.max)\
                          .then_inc(window1_added, 1)
            walk_edges(dve, 3, edges1)

            def outs(step):
                if (c := step.item(0)):
                    at, slot, turn = c
                    wait(dve, e_spread, at - 1)
                    nc.vector.tensor_scalar(degree[D:D + 1, slot, :], sum_feat[D:D + 1, bass.ds(at * CHUNK, CHUNK)],
                                            1.0, None, ALU.max).then_inc(e_degree, 1)
                    wait(dve, e_degree, at + 1)
                    nc.vector.reciprocal(degree[D:D + 1, slot, :], degree[D:D + 1, slot, :]).then_inc(e_recip, 1)
                if (c := step.item(1)):
                    at, slot, turn = c
                    wait(dve, e_spread, at + 1)
                    wait(dve, e_out, at - 1)
                    nc.vector.tensor_tensor(mean_chunk[0:D, slot, :], sum_feat[0:D, bass.ds(at * CHUNK, CHUNK)],
                                            ps[0:D, slot, :], ALU.mult).then_inc(e_mean, 1)
                if (c := step.item(2)):
                    at, slot, turn = c
                    wait(dve, e_kept, at + 1)
                    hold(dve, dve_passed)
                    width = LAST if isinstance(at, int) and at == NCH - 1 else CHUNK
                    for k, kept in enumerate((sum_feat, max_feat)):
                        nc.vector.bn_stats(bn_stats[:, k, bass.ds(at, 1), :].rearrange("p a f -> p (a f)"),
                                           kept[0:D, bass.ds(at * CHUNK, width)]).then_inc(e_stats, 1)
            walk_nodes(dve, 2, outs)

            dve.wait_ge(e_stats, 2 * NCH)
            for k in range(2):
                nc.vector.bn_aggr(bn_mv[:, k, :], bn_stats[:, k, :, :]).then_inc(e_bn, 1)
            dve.wait_ge(e_bn, 2)
            dve.wait_ge(e_pow, 2)
            nc.vector.tensor_tensor(bn_a[:, :], bn_scale[:, :], bn_rstd[:, :], ALU.mult).then_inc(e_bn, 1)
            dve.wait_ge(e_bn, 3)
            nc.vector.tensor_tensor(bn_am[:, :], bn_a[:, :], bn_mv[:, :, 0], ALU.mult).then_inc(e_bn, 1)
            dve.wait_ge(e_bn, 4)
            nc.vector.tensor_tensor(bn_am[:, :], bn_shift[:, :], bn_am[:, :], ALU.subtract).then_inc(e_bn, 1)
            dve.wait_ge(e_bn, 5)
            nc.vector.tensor_tensor(bn_c[:, 2:3], bn_am[:, 0:1], bn_am[:, 1:2], ALU.add).then_inc(e_bn, 3)
            dve.wait_ge(e_kept, NCH)

            def finish(step):
                if (c := step.item(0)):
                    at, slot, turn = c
                    wait(dve, f_shift, at + 1)
                    nc.vector.scalar_tensor_tensor(out=shifted[:, slot, :],
                                                   in0=max_feat[:, bass.ds(at * CHUNK, CHUNK)], scalar=bn_a[:, 1:2],
                                                   in1=shifted[:, slot, :], op0=ALU.mult, op1=ALU.add)\
                      .then_inc(f_sum, 1)
                if (c := step.item(1)):
                    at, slot, turn = c
                    wait(dve, f_sum, at + 1)
                    wait(dve, f_turned, at - 1)
                    nc.vector.scalar_tensor_tensor(out=y_chunk[0:D, slot, :], in0=shifted[:, slot, :], scalar=0.01,
                                                   in1=shifted[:, slot, :], op0=ALU.mult, op1=ALU.max)\
                      .then_inc(f_leaky, 1)
                if (c := step.item(2)):
                    at, slot, turn = c
                    wait(dve, f_turned, at + 1)
                    wait(dve, f_stored[slot], turn * 16)
                    nc.vector.tensor_tensor(y_tile[:, slot, :, :],
                                            ps[:, 6 + slot, 0:4 * D].rearrange("p (t f) -> p t f", f=D),
                                            x_nodes[:, bass.ds(at * 4, 4), :], ALU.add).then_inc(f_added, 1)
            walk_nodes(dve, 2, finish)


_WEIGHTS = ["L0_gnn_mW1", "L0_gnn_mb1", "L0_gnn_mW2", "L0_gnn_mb2", "L0_gnn_gW1", "L0_gnn_gb1", "L0_gnn_gW2",
            "L0_gnn_gb2", "L0_gnn_uW1", "L0_gnn_ub1", "L0_gnn_uW2", "L0_gnn_ub2", "L0_gnn_ln_g", "L0_gnn_ln_b",
            "L1_gnn_W_self1", "L1_gnn_W_neigh1", "L1_gnn_W_pool", "L1_gnn_b_pool", "L1_gnn_W_self2",
            "L1_gnn_W_neigh2", "L1_gnn_g1", "L1_gnn_beta1", "L1_gnn_g2", "L1_gnn_beta2"]


def kernel(**inputs):
    import numpy as _np
    import concourse.bacc as _bacc
    from concourse import mybir as _mybir
    from concourse.bass_utils import run_bass_kernel_spmd as _run

    def lanes(v):
        return v.reshape(ET, P).T

    src = _np.pad(_np.asarray(inputs["src"]), (0, EPAD - E))
    dst = _np.pad(_np.asarray(inputs["dst"]), (1, EPAD - E + 1), constant_values=(-1, N))
    laid = {
        "x": _np.pad(_np.asarray(inputs["x"]), ((0, NPAD - N), (0, 0))).reshape(NT, P, D).transpose(1, 0, 2),
        "src_lanes": lanes(src),
        "dst_lanes": lanes(dst[1:EPAD + 1]),
        "dst_next_lanes": lanes(dst[2:EPAD + 2]),
        "dst_ext": dst[0:EPAD + 1],
        "edge_attr_t": _np.pad(_np.asarray(inputs["edge_attr_32"]), ((0, EPAD - E), (0, 0))).T,
    }
    for name in _WEIGHTS:
        laid[name] = _np.asarray(inputs[name])
    nc = _bacc.Bacc("TRN2", target_bir_lowering=False, num_devices=1)
    arrays, args = {}, []
    for name, a in laid.items():
        a = _np.ascontiguousarray(a)
        arrays[f"in_{name}"] = a
        args.append(nc.dram_tensor(f"in_{name}", a.shape, _mybir.dt.from_np(a.dtype), kind="ExternalInput").ap())
    args.append(nc.dram_tensor("out_0", (P, NT, D), _mybir.dt.float32, kind="ExternalOutput").ap())
    gnn(nc, *args)
    r = _run(nc, [arrays], core_ids=[0])
    return r.results[0]["out_0"].transpose(1, 0, 2).reshape(NPAD, D)[0:N]
```

```python
from contextlib import ExitStack

import concourse.bass as bass
from concourse import mybir

F32 = mybir.dt.float32
I32 = mybir.dt.int32
ALU = mybir.AluOpType
ACT = mybir.ActivationFunctionType

P = 128
N, E, D, DE = 6250, 106250, 96, 32
GROUP = 4
CHUNK = 4 * P
NCH = -(-N // CHUNK)
NPAD = NCH * CHUNK
NT = NPAD // P
LAST = N - (NCH - 1) * CHUNK
ET = -(-E // (P * GROUP)) * GROUP
EPAD = ET * P
NG = ET // GROUP
RING = 4
ROW0 = 2 * D
ROW1 = 2 * D + 1
BN_EPS = LN_EPS = 1e-5


class Step:

    def __init__(self, turn, slot, unroll, count):
        self.turn, self.slot, self.unroll, self.count = turn, slot, unroll, count

    def item(self, lag=0):
        slot, turn = self.slot - lag, self.turn
        while slot < 0:
            slot, turn = slot + self.unroll, turn - 1
        at = turn * self.unroll + slot
        if isinstance(at, int) and not 0 <= at < self.count:
            return None
        return at, slot, turn


def walk(engine, count, lags, unroll, peeled, body):
    for s in range(peeled):
        body(Step(s // unroll, s % unroll, unroll, count))
    with engine.Fori(peeled // unroll, count // unroll) as turn:
        for k in range(unroll):
            body(Step(turn, k, unroll, count))
    for s in range(count // unroll * unroll, count + lags):
        body(Step(s // unroll, s % unroll, unroll, count))


def walk_edges(engine, lags, body):
    walk(engine, NG, lags, RING, 2 * RING, body)


def walk_nodes(engine, lags, body):
    walk(engine, NCH, lags, 2, 6, body)


def wait(engine, sem, value):
    if not isinstance(value, int) or value > 0:
        engine.wait_ge(sem, value)


def hold(engine, passed):
    engine.sem_inc(passed, 1)


def gnn(nc, x, src_lanes, dst_lanes, dst_next_lanes, dst_ext, edge_attr_t,
        mW1, mb1, mW2, mb2, gW1, gb1, gW2, gb2, uW1, ub1, uW2, ub2, ln_g, ln_b,
        W_self1, W_neigh1, W_pool, b_pool, W_self2, W_neigh2, g1, beta1, g2, beta2, out):
    with ExitStack() as ctx:
        def sb(name, shape, dt=F32):
            return ctx.enter_context(nc.sbuf_tensor(name, shape, dt))

        def sem(name):
            return ctx.enter_context(nc.semaphore(name))

        def sems(name, n):
            return [sem(f"{name}{i}") for i in range(n)]

        table0 = nc.dram_tensor("table0", (NPAD, ROW0), F32)
        table1 = nc.dram_tensor("table1", (NPAD, ROW1), F32)
        same_dst = nc.dram_tensor("same_dst", (EPAD,), F32)
        inv_degree = nc.dram_tensor("inv_degree", (NPAD,), F32)

        x_nodes = sb("x_nodes", [P, NT, D])
        h_nodes = sb("h_nodes", [P, NT, D])
        h_feat = sb("h_feat", [D + 1, NPAD])
        sum_feat = sb("sum_feat", [D + 1, NPAD])
        max_feat = sb("max_feat", [D, NPAD])

        rows = sb("rows", [P, RING, GROUP * ROW1])
        indices = sb("indices", [P, RING, GROUP], I32)
        stream = sb("stream", [D, RING, GROUP * P])
        pre = sb("pre", [P, 2, GROUP * ROW0])
        gate_act = sb("gate_act", [P, 2, GROUP, D])
        msg = sb("msg", [P, 2, GROUP, D + 1])
        logit = sb("logit", [P, 2, GROUP])
        tanh = sb("tanh", [P, 2, GROUP])
        gate = sb("gate", [P, 2, GROUP])
        onehot = sb("onehot", [P, RING, GROUP, P])
        scanned = sb("scanned", [D, 2, GROUP * P])
        ends = sb("ends", [P, 2, GROUP, D])

        h_tile = sb("h_tile", [P, 2, 4, D])
        h_chunk = sb("h_chunk", [D + 1, 2, CHUNK])
        u_chunk = sb("u_chunk", [D + 1, 2, CHUNK])
        y_tile = sb("y_tile", [P, 2, 4, D])
        out_rows = sb("out_rows", [P, 2, 4 * ROW1])
        mean_chunk, shifted, y_chunk = u_chunk, scanned, h_chunk
        stats = sb("stats", [P, 2, 4, 6])
        mv = sb("mv", [P, 2, 4, 2])
        rstd = sb("rstd", [P, 2, 4])
        nmr = sb("nmr", [P, 2, 4])
        var_eps = sb("var_eps", [P, 4])
        var_eps2 = sb("var_eps2", [P, 4])
        power = sb("power", [P, 4])
        degree = sb("degree", [P, NT])

        dst_i = sb("dst_i", [P, ET], I32)
        dst_rel = sb("dst_rel", [P, ET])
        is_end = sb("is_end", [P, ET])

        ident = sb("ident", [P, P])
        columns = sb("columns", [P, P])
        lane = sb("lane", [P, 1])
        ones = sb("ones", [P, P])
        w_table0 = sb("w_table0", [D + 1, ROW0])
        w_edge = sb("w_edge", [DE, ROW0])
        w_gate = sb("w_gate", [P, D])
        b_gate = sb("b_gate", [P, 1])
        w_m2 = sb("w_m2", [D, D])
        w_m2t = sb("w_m2t", [D, D + 1])
        w_u1_agg = sb("w_u1_agg", [D, D])
        w_u1_h = sb("w_u1_h", [D + 1, D])
        w_u1_sum = sb("w_u1_sum", [D + 1, D])
        w_u2 = sb("w_u2", [D + 1, D])
        scale_ln = sb("scale_ln", [P, D])
        shift_ln = sb("shift_ln", [P, D])
        w_pool = sb("w_pool", [D + 1, D])
        w_self = sb("w_self", [D, 2, D])
        w_neigh = sb("w_neigh", [D, 2, D])
        bn_scale = sb("bn_scale", [D, 2])
        bn_shift = sb("bn_shift", [D, 2])
        bn_stats = sb("bn_stats", [D, 2, NCH, 6])
        bn_mv = sb("bn_mv", [D, 2, 2])
        bn_rstd = sb("bn_rstd", [D, 2])
        bn_a = sb("bn_a", [D, 2])
        bn_am = sb("bn_am", [D, 2])
        bn_c = sb("bn_c", [D, 3])

        ps = ctx.enter_context(nc.psum_tensor("ps", [P, 8, 512], F32))

        edges_loaded = sem("edges_loaded")
        pool_passed = sem("pool_passed")
        dve_passed = sem("dve_passed")
        weights_loaded = sem("weights_loaded")
        x_loaded = sems("x_loaded", 3)
        consts_made = sem("consts_made")
        columns_made = sem("columns_made")
        cleared = sem("cleared")
        biases_made = sem("biases_made")
        same_made = sem("same_made")
        same_stored = sem("same_stored")
        dst_float = sem("dst_float")
        base_spread = sem("base_spread")
        dst_ready = sem("dst_ready")
        sums_zero = sem("sums_zero")
        m2_turned = sem("m2_turned")
        m2_copied = sem("m2_copied")
        u1_product = sem("u1_product")
        u1_ready = sem("u1_ready")
        a_bn = sem("a_bn")
        a_stats = sem("a_stats")
        a_eps = sem("a_eps")
        a_rstd = sem("a_rstd")
        a_nmr = sem("a_nmr")
        a_h = sem("a_h")
        a_turned = sem("a_turned")
        a_copied = sem("a_copied")
        a_kept = sem("a_kept")
        a_shifted = sem("a_shifted")
        a_product = sem("a_product")
        a_evac = sem("a_evac")
        a_stored = sems("a_stored", 2)
        attr_loaded = sems("attr_loaded", RING)
        index_loaded = sems("index_loaded", RING)
        gathered = sems("gathered", RING)
        pre_product = sem("pre_product")
        pre_added = sem("pre_added")
        gate_gelu = sem("gate_gelu")
        msg_gelu = sem("msg_gelu")
        logits_done = sem("logits_done")
        tanh_done = sem("tanh_done")
        gate_done = sem("gate_done")
        onehot_done = sem("onehot_done")
        summed = sem("summed")
        window_added = sem("window_added")
        c_u = sem("c_u")
        c_gelu = sem("c_gelu")
        c_update = sem("c_update")
        c_hs = sem("c_hs")
        c_bn = sem("c_bn")
        c_stats = sem("c_stats")
        c_eps = sem("c_eps")
        c_rstd = sem("c_rstd")
        c_ln = sem("c_ln")
        c_bn2 = sem("c_bn2")
        c_stats2 = sem("c_stats2")
        c_eps2 = sem("c_eps2")
        c_rstd2 = sem("c_rstd2")
        c_nmr = sem("c_nmr")
        c_h = sem("c_h")
        c_turned = sem("c_turned")
        c_copied = sem("c_copied")
        c_kept = sem("c_kept")
        c_pool = sem("c_pool")
        c_evac = sem("c_evac")
        c_stored = sems("c_stored", 2)
        mask_loaded = sems("mask_loaded", RING)
        index1_loaded = sems("index1_loaded", RING)
        gathered1 = sems("gathered1", RING)
        sums_cleared = sem("sums_cleared")
        turned = sem("turned")
        scan_done = sem("scan_done")
        onehot1_done = sem("onehot1_done")
        turned_back = sem("turned_back")
        ends_done = sem("ends_done")
        picked = sem("picked")
        rows_summed = sem("rows_summed")
        sums_added = sem("sums_added")
        maxima_added = sem("maxima_added")
        degree_moved = sem("degree_moved")
        degree_inverted = sem("degree_inverted")
        inverse_stored = sem("inverse_stored")
        inverse_loaded = sems("inverse_loaded", 2)
        e_mean = sem("e_mean")
        e_out = sem("e_out")
        e_stats = sem("e_stats")
        e_kept = sem("e_kept")
        e_bn = sem("e_bn")
        e_pow = sem("e_pow")
        f_shift = sem("f_shift")
        f_sum = sem("f_sum")
        f_leaky = sem("f_leaky")
        f_turned = sem("f_turned")
        f_added = sem("f_added")
        f_stored = sems("f_stored", 2)

        block = ctx.enter_context(nc.Block())

        staging = rows[:, :, :].rearrange("p a b -> p (a b)").bitcast(I32)
        row_dst = staging[:, 0:ET]
        row_prev = staging[:, ET:2 * ET]
        next_i = is_end[:, :].bitcast(I32)
        same = onehot[:, :, :, :].rearrange("p a b c -> p (a b c)")[:, 0:ET]
        N_EDGE_LOADS, N_WEIGHT_LOADS = 4, 27
        X_PIECES = ((0, 1), (1, 4), (4, NCH))

        def rows0(slot):
            return rows[:, slot, 0:GROUP * ROW0]

        def tile_rows(t):
            return t.rearrange("(t p) f -> p t f", p=P)

        @block.sync
        def _(sp):
            for k, (a, b) in enumerate(X_PIECES):
                sp.dma_start(x_nodes[:, a * 4:b * 4, :], x[:, a * 4:b * 4, :]).then_inc(x_loaded[k], 16)
            sp.dma_start(row_dst, dst_ext[1:EPAD + 1].rearrange("(p t) -> p t", p=P)).then_inc(edges_loaded, 16)
            sp.dma_start(row_prev, dst_ext[0:EPAD].rearrange("(p t) -> p t", p=P)).then_inc(edges_loaded, 16)
            sp.dma_start(dst_i[:, :], dst_lanes).then_inc(edges_loaded, 16)
            sp.dma_start(next_i, dst_next_lanes).then_inc(edges_loaded, 16)

            def store0(step):
                if (c := step.item(3)):
                    at, slot, turn = c
                    wait(sp, a_evac, at + 1)
                    sp.dma_start(tile_rows(table0)[:, bass.ds(at * 4, 4), :],
                                 pre[:, slot, :].rearrange("p (t f) -> p t f", f=ROW0)).then_inc(a_stored[slot], 16)
            walk_nodes(sp, 3, store0)
            sp.wait_ge(same_made, 1)
            sp.dma_start(same_dst.rearrange("(p t) -> p t", p=P), same).then_inc(same_stored, 16)

            def load0(step):
                at, slot, turn = step.item()
                wait(sp, gathered[slot], turn * 64)
                sp.dma_start(indices[:, slot, :], src_lanes[:, bass.ds(at * GROUP, GROUP)])\
                  .then_inc(index_loaded[slot], 16)
                wait(sp, pre_product, at - RING + 1)
                sp.dma_start(stream[0:DE, slot, :], edge_attr_t[:, bass.ds(at * CHUNK, CHUNK)])\
                  .then_inc(attr_loaded[slot], 16)
            walk_edges(sp, 0, load0)

            def store1(step):
                if (c := step.item(4)):
                    at, slot, turn = c
                    wait(sp, c_evac, at + 1)
                    sp.dma_start(tile_rows(table1)[:, bass.ds(at * 4, 4), :],
                                 out_rows[:, slot, :].rearrange("p (t f) -> p t f", f=ROW1))\
                      .then_inc(c_stored[slot], 16)
            walk_nodes(sp, 4, store1)

            sp.wait_ge(same_stored, 16)
            sp.wait_ge(pre_product, NG)
            for slot in range(RING):
                sp.wait_ge(gathered[slot], 64 * (NG // RING))

            def load1(step):
                at, slot, turn = step.item()
                wait(sp, gathered1[slot], turn * 64)
                sp.dma_start(indices[:, slot, :], src_lanes[:, bass.ds(at * GROUP, GROUP)])\
                  .then_inc(index1_loaded[slot], 16)
                wait(sp, scan_done, at - RING + 1)
                sp.dma_start(stream[:, slot, :],
                             same_dst[bass.ds(at * CHUNK, CHUNK)].partition_broadcast(D))\
                  .then_inc(mask_loaded[slot], 16)
            walk_edges(sp, 0, load1)

            sp.wait_ge(sums_added, ET)
            sp.dma_start(degree[:, :], sum_feat[D:D + 1, :].rearrange("a (p t) -> a p t", p=P)).then_inc(degree_moved, 16)
            sp.wait_ge(degree_inverted, 2)
            sp.dma_start(inv_degree.rearrange("(p t) -> p t", p=P), degree[:, :]).then_inc(inverse_stored, 16)
            sp.wait_ge(inverse_stored, 16)

            def load_inverse(step):
                at, slot, turn = step.item()
                wait(sp, e_mean, at - 1)
                sp.dma_start(stream[:, slot, :],
                             inv_degree[bass.ds(at * CHUNK, CHUNK)].partition_broadcast(D))\
                  .then_inc(inverse_loaded[slot], 16)
            walk_nodes(sp, 0, load_inverse)

            def store_out(step):
                if (c := step.item(3)):
                    at, slot, turn = c
                    wait(sp, f_added, at + 1)
                    sp.dma_start(out[:, bass.ds(at * 4, 4), :], y_tile[:, slot, :, :]).then_inc(f_stored[slot], 16)
            walk_nodes(sp, 3, store_out)
            sp.wait_ge(f_stored[0], 16 * ((NCH + 1) // 2))
            sp.wait_ge(f_stored[1], 16 * (NCH // 2))



        @block.gpsimd
        def _(pool):
            nc.gpsimd.memset(power[:, :], -0.5).then_inc(consts_made, 1)
            nc.gpsimd.memset(ident[:, :], 0.0).then_inc(consts_made, 1)
            nc.gpsimd.memset(ones[:, :], 1.0).then_inc(consts_made, 1)
            pool.wait_ge(consts_made, 3)
            nc.gpsimd.affine_select(out=ident[:, :], in_=ident[:, :], compare_op=ALU.not_equal, fill=1.0,
                                    base=0, pattern=[[-1, P]], channel_multiplier=1).then_inc(consts_made, 1)
            nc.gpsimd.iota(columns[:, :], [[1, P]], 0, 0, allow_small_or_imprecise_dtypes=True)\
              .then_inc(columns_made, 1)
            nc.gpsimd.iota(lane[:, :], [[0, 1]], 0, 1, allow_small_or_imprecise_dtypes=True)\
              .then_inc(columns_made, 1)
            pool.wait_ge(columns_made, 2)

            def prepare(step):
                if (c := step.item(0)):
                    at, slot, turn = c
                    wait(pool, a_stats, at + 1)
                    wait(pool, a_rstd, at)
                    hold(pool, pool_passed)
                    nc.gpsimd.tensor_scalar(var_eps[:, :], mv[:, slot, :, 1], LN_EPS, None, ALU.add)\
                      .then_inc(a_eps, 1)
                    wait(pool, a_eps, at + 1)
                    wait(pool, a_nmr, at - 1)
                    wait(pool, a_h, at - 1)
                    nc.gpsimd.tensor_tensor(rstd[:, slot, :], var_eps[:, :], power[:, :], ALU.pow)\
                      .then_inc(a_rstd, 1)
                if (c := step.item(2)):
                    at, slot, turn = c
                    wait(pool, a_h, at + 1)
                    if isinstance(at, int) and at == 0:
                        pool.wait_ge(weights_loaded, 16 * N_WEIGHT_LOADS)
                    hold(pool, pool_passed)
                    chunk = x_nodes[:, bass.ds(at * 4, 4), :]
                    nc.gpsimd.tensor_tensor(chunk, chunk, shift_ln[:, :].unsqueeze(1).to_broadcast([P, 4, D]), ALU.add)\
                      .then_inc(a_shifted, 1)
            walk_nodes(pool, 2, prepare)
            pool.wait_ge(a_shifted, NCH)
            nc.gpsimd.memset(h_feat[D:D + 1, :], 1.0).then_inc(biases_made, 1)

            pool.wait_ge(a_stored[0], 16 * ((NCH + 1) // 2))
            pool.wait_ge(a_stored[1], 16 * (NCH // 2))
            pool.wait_ge(same_made, 1)

            def gather0(step):
                at, slot, turn = step.item()
                wait(pool, index_loaded[slot], (turn + 1) * 16)
                wait(pool, pre_added, at - RING + 1)
                hold(pool, pool_passed)
                for j in range(GROUP):
                    nc.gpsimd.indirect_dma_start(
                        rows[:, slot, j * ROW0:(j + 1) * ROW0], None, table0[:, :],
                        bass.IndirectOffsetOnAxis(ap=indices[:, slot, j:j + 1], axis=0)).then_inc(gathered[slot], 16)
            walk_edges(pool, 0, gather0)

            def update(step):
                if (c := step.item(1)):
                    at, slot, turn = c
                    wait(pool, c_stats, at + 1)
                    wait(pool, c_rstd, at)
                    hold(pool, pool_passed)
                    nc.gpsimd.tensor_scalar(var_eps[:, :], mv[:, slot, :, 1], LN_EPS, None, ALU.add)\
                      .then_inc(c_eps, 1)
                    wait(pool, c_eps, at + 1)
                    wait(pool, c_h, at - 1)
                    nc.gpsimd.tensor_tensor(rstd[:, slot, :], var_eps[:, :], power[:, :], ALU.pow)\
                      .then_inc(c_rstd, 1)
                if (c := step.item(2)):
                    at, slot, turn = c
                    wait(pool, c_stats2, at + 1)
                    wait(pool, c_rstd2, at)
                    hold(pool, pool_passed)
                    nc.gpsimd.tensor_scalar(var_eps2[:, :], mv[:, slot, :, 1], LN_EPS, None, ALU.add)\
                      .then_inc(c_eps2, 1)
                    wait(pool, c_eps2, at + 1)
                    nc.gpsimd.tensor_tensor(rstd[:, slot, :], var_eps2[:, :], power[:, :], ALU.pow)\
                      .then_inc(c_rstd2, 1)
            walk_nodes(pool, 2, update)

            pool.wait_ge(c_stored[0], 16 * ((NCH + 1) // 2))
            pool.wait_ge(c_stored[1], 16 * (NCH // 2))

            def gather1(step):
                at, slot, turn = step.item()
                wait(pool, index1_loaded[slot], (turn + 1) * 16)
                wait(pool, rows_summed, at - RING + 1)
                hold(pool, pool_passed)
                for j in range(GROUP):
                    nc.gpsimd.indirect_dma_start(
                        rows[:, slot, j * ROW1:(j + 1) * ROW1], None, table1[:, :],
                        bass.IndirectOffsetOnAxis(ap=indices[:, slot, j:j + 1], axis=0)).then_inc(gathered1[slot], 16)
            walk_edges(pool, 0, gather1)

            pool.wait_ge(e_bn, 2)
            nc.gpsimd.tensor_scalar(bn_c[:, 0:2], bn_mv[:, :, 1], BN_EPS, None, ALU.add).then_inc(e_pow, 1)
            pool.wait_ge(e_pow, 1)
            nc.gpsimd.tensor_tensor(bn_rstd[:, :], bn_c[:, 0:2], power[0:D, 0:2], ALU.pow).then_inc(e_pow, 1)

        @block.scalar
        def _(act):
            def load(to, of):
                act.dma_start(to, of).then_inc(weights_loaded, 16)

            def row(v):
                return v.rearrange("(a n) -> a n", a=1)

            def col(v):
                return v.rearrange("(n a) -> n a", a=1)

            load(w_table0[0:D, 0:D], mW1[0:D, :])
            load(w_table0[0:D, D:ROW0], gW1[0:D, :])
            load(w_table0[D:D + 1, 0:D], row(mb1))
            load(w_table0[D:D + 1, D:ROW0], row(gb1))
            load(w_edge[:, 0:D], mW1[D:D + DE, :])
            load(w_edge[:, D:ROW0], gW1[D:D + DE, :])
            load(w_gate[:, :], gW2.rearrange("n a -> (n a)").partition_broadcast(P))
            load(b_gate[:, :], gb2.partition_broadcast(P))
            load(w_m2[:, :], mW2)
            load(w_m2t[:, D:D + 1], col(mb2))
            load(w_u1_h[0:D, :], uW1[0:D, :])
            load(w_u1_h[D:D + 1, :], row(ub1))
            load(w_u1_agg[:, :], uW1[D:2 * D, :])
            load(w_u2[0:D, :], uW2)
            load(w_u2[D:D + 1, :], row(ub2))
            load(scale_ln[:, :], ln_g.partition_broadcast(P))
            load(shift_ln[:, :], ln_b.partition_broadcast(P))
            load(w_pool[0:D, :], W_pool)
            load(w_pool[D:D + 1, :], row(b_pool))
            for k, (s, n, g, b) in enumerate(((W_self1, W_neigh1, g1, beta1), (W_self2, W_neigh2, g2, beta2))):
                load(w_self[:, k, :], s)
                load(w_neigh[:, k, :], n)
                load(bn_scale[:, k:k + 1], col(g))
            act.dma_start(bn_shift[:, 0:1], col(beta1)).then_inc(weights_loaded, 16)
            act.dma_start(bn_shift[:, 1:2], col(beta2)).then_inc(weights_loaded, 16)

            def prepare(step):
                if (c := step.item(1)):
                    at, slot, turn = c
                    wait(act, a_nmr, at + 1)
                    wait(act, a_turned, at - 1)
                    wait(act, a_kept, 2 * (at - 1))
                    for j in range(4):
                        last = nc.scalar.activation(h_tile[:, slot, j, :], x_nodes[:, bass.ds(at * 4 + j, 1), :]
                                                    .rearrange("p a f -> p (a f)"), ACT.Relu,
                                                    bias=nmr[:, slot, j:j + 1], scale=rstd[:, slot, j:j + 1])
                    last.then_inc(a_h, 1)
                if (c := step.item(3)):
                    at, slot, turn = c
                    wait(act, a_product, at + 1)
                    wait(act, a_stored[slot], turn * 16)
                    nc.scalar.activation(pre[:, slot, :].rearrange("p (b f) -> p b f", b=2),
                                         ps[:, 2 + 2 * slot:4 + 2 * slot, 0:2 * ROW0], ACT.Copy).then_inc(a_evac, 1)
            walk_nodes(act, 3, prepare)

            act.wait_ge(a_stored[0], 16 * ((NCH + 1) // 2))
            act.wait_ge(a_stored[1], 16 * (NCH // 2))

            def edges0(step):
                if (c := step.item(1)):
                    at, slot, turn = c
                    wait(act, logits_done, at + 1)
                    wait(act, gate_done, at - 1)
                    nc.scalar.activation(tanh[:, slot % 2, :], logit[:, slot % 2, :], ACT.Tanh,
                                         bias=b_gate[:, 0:1], scale=0.5).then_inc(tanh_done, 1)
                if (c := step.item(0)):
                    at, slot, turn = c
                    z = pre[:, slot % 2, :].rearrange("p (t k f) -> p t k f", t=GROUP, k=2)
                    wait(act, pre_added, at + 1)
                    wait(act, logits_done, at - 1)
                    nc.scalar.activation(gate_act[:, slot % 2, :, :], z[:, :, 1, :], ACT.Gelu).then_inc(gate_gelu, 1)
                    wait(act, summed, at - 1)
                    nc.scalar.activation(msg[:, slot % 2, :, 0:D], z[:, :, 0, :], ACT.Gelu).then_inc(msg_gelu, 1)
            act.wait_ge(u1_ready, 1)
            walk_edges(act, 1, edges0)

            act.wait_ge(sums_zero, 7)

            def update(step):
                if (c := step.item(3)):
                    at, slot, turn = c
                    wait(act, c_nmr, at + 1)
                    wait(act, c_stored[slot], turn * 16)
                    for j in range(4):
                        last = nc.scalar.activation(out_rows[:, slot, j * ROW1:j * ROW1 + D],
                                                    x_nodes[:, bass.ds(at * 4 + j, 1), :]
                                                    .rearrange("p a f -> p (a f)"), ACT.Relu,
                                                    bias=nmr[:, slot, j:j + 1], scale=rstd[:, slot, j:j + 1])
                    last.then_inc(c_h, 1)
                if (c := step.item(0)):
                    at, slot, turn = c
                    wait(act, c_u, at + 1)
                    wait(act, c_update, at - 1)
                    nc.scalar.activation(u_chunk[0:D, slot, :], ps[0:D, slot, :], ACT.Gelu).then_inc(c_gelu, 1)
                if (c := step.item(4)):
                    at, slot, turn = c
                    wait(act, c_pool, at + 1)
                    nc.scalar.activation(out_rows[:, slot, :].rearrange("p (t f) -> p t f", f=ROW1)[:, :, D + 1:ROW1],
                                         ps[:, 6 + slot, 0:4 * D].rearrange("p (t f) -> p t f", f=D), ACT.Relu)\
                      .then_inc(c_evac, 1)
            walk_nodes(act, 4, update)

            def edges1(step):
                if (c := step.item(1)):
                    at, slot, turn = c
                    wait(act, turned_back, at + 1)
                    wait(act, picked, at - 1)
                    for j in range(GROUP):
                        last = nc.scalar.activation(ends[:, slot % 2, j, :], ps[:, 2 + slot % 2, j * D:(j + 1) * D],
                                                    ACT.Copy, scale=is_end[:, bass.ds(at * GROUP + j, 1)])
                    last.then_inc(ends_done, 1)
            walk_edges(act, 1, edges1)

            def outs(step):
                if (c := step.item(2)):
                    at, slot, turn = c
                    wait(act, e_out, at + 1)
                    nc.scalar.activation(sum_feat[0:D, bass.ds(at * CHUNK, CHUNK)], ps[0:D, 2 + slot, :], ACT.Copy)
                    nc.scalar.activation(max_feat[:, bass.ds(at * CHUNK, CHUNK)], ps[0:D, 4 + slot, :], ACT.Copy)\
                      .then_inc(e_kept, 1)
            walk_nodes(act, 2, outs)

            act.wait_ge(e_bn, 8)

            def finish(step):
                if (c := step.item(0)):
                    at, slot, turn = c
                    wait(act, f_leaky, at - 1)
                    nc.scalar.activation(shifted[:, slot, :], sum_feat[0:D, bass.ds(at * CHUNK, CHUNK)], ACT.Identity,
                                         bias=bn_c[:, 2:3], scale=bn_a[:, 0:1]).then_inc(f_shift, 1)
            walk_nodes(act, 0, finish)

        @block.tensor
        def _(pe):
            pe.wait_ge(consts_made, 4)
            pe.wait_ge(weights_loaded, 16 * N_WEIGHT_LOADS)
            pe.wait_ge(cleared, 2)

            def prepare(step):
                if (c := step.item(1)):
                    at, slot, turn = c
                    wait(pe, a_h, at + 1)
                    wait(pe, a_copied, at - 1)
                    for j in range(4):
                        last = nc.tensor.transpose(ps[0:D, slot, j * P:(j + 1) * P], h_tile[:, slot, j, :], ident[:, :])
                    last.then_inc(a_turned, 1)
                if (c := step.item(2)):
                    at, slot, turn = c
                    wait(pe, a_copied, at + 1)
                    wait(pe, a_evac, at - 1)
                    for j in range(4):
                        last = nc.tensor.matmul(ps[:, 2 + 2 * slot + j // 2, (j % 2) * ROW0:(j % 2 + 1) * ROW0],
                                                h_chunk[:, slot, j * P:(j + 1) * P], w_table0[:, :],
                                                start=True, stop=True)
                    last.then_inc(a_product, 1)
            walk_nodes(pe, 2, prepare)

            pe.wait_ge(dst_float, 1)
            half = ET // 2
            for k in range(2):
                last = nc.tensor.matmul(ps[:, 6 + k, 0:half], ones[0:1, :], dst_rel[0:1, k * half:(k + 1) * half],
                                        start=True, stop=True)
            last.then_inc(base_spread, 1)

            pe.wait_ge(dst_ready, 3)
            nc.tensor.transpose(ps[0:D, 6, 0:D], w_m2[:, :], ident[0:D, 0:D]).then_inc(m2_turned, 1)
            pe.wait_ge(m2_copied, 1)
            nc.tensor.matmul(ps[0:D + 1, 7, 0:D], w_m2t[:, :], w_u1_agg[:, :], start=True, stop=True)\
              .then_inc(u1_product, 1)

            pe.wait_ge(a_evac, NCH)
            pe.wait_ge(a_copied, NCH)

            def edges0(step):
                if (c := step.item(0)):
                    at, slot, turn = c
                    wait(pe, attr_loaded[slot], (turn + 1) * 16)
                    wait(pe, pre_added, at - 1)
                    for j in range(GROUP):
                        last = nc.tensor.matmul(
                            ps[:, 2 * (slot % 2) + j // 2, (j % 2) * ROW0:(j % 2 + 1) * ROW0],
                            stream[0:DE, slot, j * P:(j + 1) * P], w_edge[:, :], start=True, stop=True)
                    last.then_inc(pre_product, 1)
                if (c := step.item(2)):
                    at, slot, turn = c
                    wait(pe, msg_gelu, at + 1)
                    wait(pe, onehot_done, at + 1)
                    wait(pe, window_added, 4 * (at - 1))
                    for j in range(GROUP):
                        last = nc.tensor.matmul(ps[0:D + 1, 4 + slot % 2, j * P:(j + 1) * P], msg[:, slot % 2, j, :],
                                                onehot[:, slot % 2, j, :], start=True, stop=True)
                    last.then_inc(summed, 1)
            walk_edges(pe, 2, edges0)

            pe.wait_ge(window_added, ET)
            pe.wait_ge(u1_ready, 2)
            pe.wait_ge(a_kept, 2 * NCH)
            pe.wait_ge(biases_made, 1)

            def update(step):
                if (c := step.item(0)):
                    at, slot, turn = c
                    wait(pe, c_gelu, at - 1)
                    nc.tensor.matmul(ps[0:D, slot, :], w_u1_h[:, :], h_feat[:, bass.ds(at * CHUNK, CHUNK)],
                                     start=True, stop=False)
                    nc.tensor.matmul(ps[0:D, slot, :], w_u1_sum[:, :], sum_feat[:, bass.ds(at * CHUNK, CHUNK)],
                                     start=False, stop=True).then_inc(c_u, 1)
                if (c := step.item(1)):
                    at, slot, turn = c
                    wait(pe, c_gelu, at + 1)
                    wait(pe, c_hs, at - 1)
                    for j in range(4):
                        last = nc.tensor.matmul(ps[:, 2 + slot, j * D:(j + 1) * D], u_chunk[:, slot, j * P:(j + 1) * P],
                                                w_u2[:, :], start=True, stop=True)
                    last.then_inc(c_update, 1)
                if (c := step.item(3)):
                    at, slot, turn = c
                    wait(pe, c_h, at + 1)
                    wait(pe, c_copied, at - 1)
                    for j in range(4):
                        last = nc.tensor.transpose(ps[0:D, 4 + slot, j * P:(j + 1) * P],
                                                   out_rows[:, slot, j * ROW1:j * ROW1 + D], ident[:, :])
                    last.then_inc(c_turned, 1)
                if (c := step.item(4)):
                    at, slot, turn = c
                    wait(pe, c_copied, at + 1)
                    wait(pe, c_evac, at - 1)
                    for j in range(4):
                        last = nc.tensor.matmul(ps[:, 6 + slot, j * D:(j + 1) * D], h_chunk[:, slot, j * P:(j + 1) * P],
                                                w_pool[:, :], start=True, stop=True)
                    last.then_inc(c_pool, 1)
            walk_nodes(pe, 4, update)

            pe.wait_ge(c_evac, NCH)
            pe.wait_ge(c_copied, NCH)
            pe.wait_ge(c_hs, NCH)

            def edges1(step):
                if (c := step.item(2)):
                    at, slot, turn = c
                    wait(pe, ends_done, at + 1)
                    wait(pe, maxima_added, GROUP * (at - 1))
                    for j in range(GROUP):
                        last = nc.tensor.matmul(ps[0:D, 6 + slot % 2, j * P:(j + 1) * P], ends[:, slot % 2, j, :],
                                                onehot[:, slot, j, :], start=True, stop=True)
                    last.then_inc(picked, 1)
                if (c := step.item(0)):
                    at, slot, turn = c
                    wait(pe, gathered1[slot], (turn + 1) * 64)
                    wait(pe, scan_done, at - 1)
                    for j in range(GROUP):
                        last = nc.tensor.transpose(ps[0:D, slot % 2, j * P:(j + 1) * P],
                                                   rows[:, slot, j * ROW1 + D + 1:(j + 1) * ROW1], ident[:, :])
                    last.then_inc(turned, 1)
                if (c := step.item(1)):
                    at, slot, turn = c
                    wait(pe, scan_done, at + 1)
                    wait(pe, ends_done, at - 1)
                    for j in range(GROUP):
                        last = nc.tensor.transpose(ps[:, 2 + slot % 2, j * D:(j + 1) * D],
                                                   scanned[:, slot % 2, j * P:(j + 1) * P], ident[0:D, 0:D])
                    last.then_inc(turned_back, 1)
                if (c := step.item(0)):
                    at, slot, turn = c
                    wait(pe, onehot1_done, at + 1)
                    wait(pe, sums_added, GROUP * (at - 1))
                    for j in range(GROUP):
                        last = nc.tensor.matmul(ps[0:D + 1, 4 + slot % 2, j * P:(j + 1) * P],
                                                rows[:, slot, j * ROW1:j * ROW1 + D + 1],
                                                onehot[:, slot, j, :], start=True, stop=True)
                    last.then_inc(rows_summed, 1)
            walk_edges(pe, 2, edges1)

            pe.wait_ge(sums_added, ET)
            pe.wait_ge(maxima_added, ET)
            pe.wait_ge(c_kept, NCH)

            def outs(step):
                at, slot, turn = step.item()
                h = h_feat[0:D, bass.ds(at * CHUNK, CHUNK)]
                wait(pe, e_kept, at - 1)
                nc.tensor.matmul(ps[0:D, 4 + slot, :], w_self[:, 1, :], h, start=True, stop=False)
                nc.tensor.matmul(ps[0:D, 4 + slot, :], w_neigh[:, 1, :], max_feat[:, bass.ds(at * CHUNK, CHUNK)],
                                 start=False, stop=True)
                nc.tensor.matmul(ps[0:D, 2 + slot, :], w_self[:, 0, :], h, start=True, stop=False)
                wait(pe, e_mean, at + 1)
                nc.tensor.matmul(ps[0:D, 2 + slot, :], w_neigh[:, 0, :], mean_chunk[0:D, slot, :],
                                 start=False, stop=True).then_inc(e_out, 1)
            walk_nodes(pe, 0, outs)

            def finish(step):
                if (c := step.item(2)):
                    at, slot, turn = c
                    wait(pe, f_leaky, at + 1)
                    wait(pe, f_added, at - 1)
                    for j in range(4):
                        last = nc.tensor.transpose(ps[:, 6 + slot, j * D:(j + 1) * D],
                                                   y_chunk[0:D, slot, j * P:(j + 1) * P], ident[0:D, 0:D])
                    last.then_inc(f_turned, 1)
            walk_nodes(pe, 2, finish)

        @block.vector
        def _(dve):
            nc.vector.memset(h_chunk[D:D + 1, :, :], 1.0).then_inc(cleared, 1)
            nc.vector.memset(u_chunk[D:D + 1, :, :], 1.0).then_inc(cleared, 1)
            nc.vector.memset(msg[:, :, :, D:D + 1], 1.0).then_inc(sums_zero, 1)

            def moments(of, slot, done, ready):
                hold(dve, dve_passed)
                for j in range(4):
                    nc.vector.bn_stats(stats[:, slot, j, :], of(j)).then_inc(done[0], 1)
                wait(dve, done[0], done[1])
                hold(dve, dve_passed)
                for j in range(4):
                    last = nc.vector.bn_aggr(mv[:, slot, j, :], stats[:, slot, j, :])
                last.then_inc(ready, 1)

            def minus_mean_rstd(slot, done):
                nc.vector.scalar_tensor_tensor(out=nmr[:, slot, :], in0=mv[:, slot, :, 0], scalar=-1.0,
                                               in1=rstd[:, slot, :], op0=ALU.mult, op1=ALU.mult).then_inc(done, 1)

            def node_tile(t, at, j):
                return t[:, bass.ds(at * 4 + j, 1), :].rearrange("p a f -> p (a f)")


            def prepare(step):
                if (c := step.item(0)):
                    at, slot, turn = c
                    wait(dve, a_nmr, at - 1)
                    if isinstance(at, int):
                        for k, (first, _) in enumerate(X_PIECES):
                            if at == first:
                                dve.wait_ge(x_loaded[k], 16)
                    moments(lambda j: node_tile(x_nodes, at, j), slot, (a_bn, 4 * at + 4), a_stats)
                if (c := step.item(1)):
                    at, slot, turn = c
                    wait(dve, a_rstd, at + 1)
                    wait(dve, a_h, at - 1)
                    minus_mean_rstd(slot, a_nmr)
                if (c := step.item(2)):
                    at, slot, turn = c
                    wait(dve, a_turned, at + 1)
                    wait(dve, a_product, at - 1)
                    nc.vector.tensor_copy(h_chunk[0:D, slot, :], ps[0:D, slot, :]).then_inc(a_copied, 1)
                    nc.vector.tensor_copy(h_nodes[:, bass.ds(at * 4, 4), :], h_tile[:, slot, :, :]).then_inc(a_kept, 1)
                    wait(dve, a_copied, at + 1)
                    nc.vector.tensor_copy(h_feat[0:D, bass.ds(at * CHUNK, CHUNK)], h_chunk[0:D, slot, :])\
                      .then_inc(a_kept, 1)
            walk_nodes(dve, 2, prepare)

            dve.wait_ge(edges_loaded, 16 * N_EDGE_LOADS)
            nc.vector.tensor_tensor(same, row_dst, row_prev, ALU.is_equal).then_inc(same_made, 1)
            nc.vector.tensor_copy(dst_rel[:, :], dst_i[:, :]).then_inc(dst_float, 1)
            nc.vector.tensor_tensor(is_end[:, :], dst_i[:, :], next_i, ALU.not_equal).then_inc(dst_float, 1)
            dve.wait_ge(columns_made, 2)
            nc.vector.tensor_scalar(lane[:, :], lane[:, :], float(P - 1), None, ALU.is_ge).then_inc(dst_float, 1)
            dve.wait_ge(dst_float, 3)
            nc.vector.tensor_scalar(is_end[:, :], is_end[:, :], lane[:, 0:1], None, ALU.max).then_inc(dst_ready, 1)
            dve.wait_ge(base_spread, 1)
            half = ET // 2
            for k in range(2):
                nc.vector.tensor_tensor(dst_rel[:, k * half:(k + 1) * half], dst_rel[:, k * half:(k + 1) * half],
                                        ps[:, 6 + k, 0:half], ALU.subtract).then_inc(dst_ready, 1)
            nc.vector.memset(sum_feat[:, :], 0.0).then_inc(sums_zero, 1)
            nc.vector.memset(max_feat[:, :], 0.0).then_inc(sums_zero, 1)
            for j in range(GROUP):
                nc.vector.memset(out_rows[:, :, j * ROW1 + D:j * ROW1 + D + 1], 1.0).then_inc(sums_zero, 1)

            dve.wait_ge(weights_loaded, 16 * N_WEIGHT_LOADS)
            dve.wait_ge(m2_turned, 1)
            nc.vector.tensor_copy(w_m2t[:, 0:D], ps[0:D, 6, 0:D]).then_inc(m2_copied, 1)
            nc.vector.tensor_scalar(b_gate[:, :], b_gate[:, :], 0.5, None, ALU.mult).then_inc(u1_ready, 1)
            dve.wait_ge(u1_product, 1)
            nc.vector.tensor_copy(w_u1_sum[:, :], ps[0:D + 1, 7, 0:D]).then_inc(u1_ready, 1)
            dve.wait_ge(sums_zero, 7)
            dve.wait_ge(same_stored, 16)

            def bases(at):
                return nc.values_load_multi_w_load_instructions(
                    dst_i[0:1, bass.ds(at * GROUP, GROUP)], engines=[mybir.EngineType.DVE], min_val=0, max_val=N,
                    skip_runtime_bounds_check_because="destinations are node numbers, the padding's is N")[1]

            def edges0(step):
                if (c := step.item(1)):
                    at, slot, turn = c
                    wait(dve, gate_gelu, at + 1)
                    wait(dve, tanh_done, at - 1)
                    for j in range(GROUP):
                        last = nc.vector.tensor_tensor_reduce(
                            out=gate_act[:, slot % 2, j, :], in0=gate_act[:, slot % 2, j, :], in1=w_gate[:, :],
                            scale=1.0, scalar=0.0, op0=ALU.mult, op1=ALU.add, accum_out=logit[:, slot % 2, j:j + 1])
                    last.then_inc(logits_done, 1)
                if (c := step.item(0)):
                    at, slot, turn = c
                    wait(dve, gathered[slot], (turn + 1) * 64)
                    wait(dve, pre_product, at + 1)
                    wait(dve, msg_gelu, at - 1)
                    nc.vector.tensor_tensor(pre[:, slot % 2, :].rearrange("p (b f) -> p b f", b=2),
                                            rows0(slot).rearrange("p (b f) -> p b f", b=2),
                                            ps[:, 2 * (slot % 2):2 * (slot % 2) + 2, 0:2 * ROW0], ALU.add)\
                      .then_inc(pre_added, 1)
                one, three = step.item(1), step.item(3)
                if one:
                    at, slot, turn = one
                    wait(dve, tanh_done, at + 1)
                    wait(dve, summed, at - 1)
                    nc.vector.tensor_scalar(gate[:, slot % 2, :], tanh[:, slot % 2, :], 0.5, 0.5, ALU.mult, ALU.add)\
                      .then_inc(gate_done, 1)
                if three:
                    wait(dve, summed, three[0] + 1)
                    base = bases(three[0])
                if one:
                    wait(dve, gate_done, one[0] + 1)
                for j in range(GROUP):
                    if one:
                        at, slot, turn = one
                        last = nc.vector.tensor_scalar(onehot[:, slot % 2, j, :], columns[:, :],
                                                       dst_rel[:, bass.ds(at * GROUP + j, 1)],
                                                       gate[:, slot % 2, j:j + 1], ALU.is_equal, ALU.mult)
                        if j == GROUP - 1:
                            last.then_inc(onehot_done, 1)
                    if three:
                        at, slot, turn = three
                        window = sum_feat[:, bass.ds(base[j], P)]
                        wait(dve, window_added, at * GROUP + j)
                        nc.vector.tensor_tensor(window, window, ps[0:D + 1, 4 + slot % 2, j * P:(j + 1) * P], ALU.add)\
                          .then_inc(window_added, 1)
            walk_edges(dve, 3, edges0)

            def update(step):
                if (c := step.item(3)):
                    at, slot, turn = c
                    wait(dve, c_rstd2, at + 1)
                    wait(dve, c_h, at - 1)
                    minus_mean_rstd(slot, c_nmr)
                if (c := step.item(1)):
                    at, slot, turn = c
                    wait(dve, c_update, at + 1)
                    nc.vector.tensor_tensor(h_tile[:, slot, :, :], ps[:, 2 + slot, 0:4 * D]
                                            .rearrange("p (t f) -> p t f", f=D),
                                            h_nodes[:, bass.ds(at * 4, 4), :], ALU.add).then_inc(c_hs, 1)
                    wait(dve, c_hs, at + 1)
                    moments(lambda j: h_tile[:, slot, j, :], slot, (c_bn, 4 * at + 4), c_stats)
                if (c := step.item(2)):
                    at, slot, turn = c
                    wait(dve, c_rstd, at + 1)
                    for j in range(4):
                        last = nc.vector.tensor_scalar(y_tile[:, slot, j, :], h_tile[:, slot, j, :],
                                                       mv[:, slot, j, 0:1], rstd[:, slot, j:j + 1],
                                                       ALU.subtract, ALU.mult)
                    last.then_inc(c_ln, 1)
                    y, chunk = y_tile[:, slot, :, :], x_nodes[:, bass.ds(at * 4, 4), :]
                    wait(dve, c_ln, 3 * at + 1)
                    nc.vector.tensor_tensor(y, y, scale_ln[:, :].unsqueeze(1).to_broadcast([P, 4, D]), ALU.mult)\
                      .then_inc(c_ln, 1)
                    wait(dve, c_ln, 3 * at + 2)
                    nc.vector.tensor_tensor(chunk, chunk, y, ALU.add).then_inc(c_ln, 1)
                    wait(dve, c_ln, 3 * at + 3)
                    moments(lambda j: node_tile(x_nodes, at, j), slot, (c_bn2, 4 * at + 4), c_stats2)
                if (c := step.item(3)):
                    at, slot, turn = c
                    wait(dve, c_turned, at + 1)
                    wait(dve, c_pool, at - 1)
                    nc.vector.tensor_copy(h_chunk[0:D, slot, :], ps[0:D, 4 + slot, :]).then_inc(c_copied, 1)
                    wait(dve, c_copied, at + 1)
                    nc.vector.tensor_copy(h_feat[0:D, bass.ds(at * CHUNK, CHUNK)], h_chunk[0:D, slot, :])\
                      .then_inc(c_kept, 1)
            dve.wait_ge(a_kept, 2 * NCH)
            dve.wait_ge(a_shifted, NCH)
            walk_nodes(dve, 3, update)

            dve.wait_ge(c_u, NCH)
            nc.vector.memset(sum_feat[:, :], 0.0).then_inc(sums_cleared, 1)
            dve.wait_ge(sums_cleared, 1)

            def edges1(step):
                zero, one, three = step.item(0), step.item(1), step.item(3)
                if one:
                    sum_base = bases(one[0])
                if three:
                    max_base = bases(three[0])
                if zero:
                    wait(dve, picked, zero[0] - RING + 1)
                if one:
                    wait(dve, rows_summed, one[0] + 1)
                if three:
                    wait(dve, picked, three[0] + 1)
                for j in range(GROUP):
                    if zero:
                        at, slot, turn = zero
                        last = nc.vector.tensor_scalar(onehot[:, slot, j, :], columns[:, :],
                                                       dst_rel[:, bass.ds(at * GROUP + j, 1)], None, ALU.is_equal)
                        if j == GROUP - 1:
                            last.then_inc(onehot1_done, 1)
                    if one:
                        at, slot, turn = one
                        window = sum_feat[:, bass.ds(sum_base[j], P)]
                        wait(dve, sums_added, at * GROUP + j)
                        nc.vector.tensor_tensor(window, window, ps[0:D + 1, 4 + slot % 2, j * P:(j + 1) * P], ALU.add)\
                          .then_inc(sums_added, 1)
                    if three:
                        at, slot, turn = three
                        window = max_feat[:, bass.ds(max_base[j], P)]
                        wait(dve, maxima_added, at * GROUP + j)
                        nc.vector.tensor_tensor(window, window, ps[0:D, 6 + slot % 2, j * P:(j + 1) * P], ALU.max)\
                          .then_inc(maxima_added, 1)
                if zero:
                    at, slot, turn = zero
                    wait(dve, turned, at + 1)
                    wait(dve, mask_loaded[slot], (turn + 1) * 16)
                    wait(dve, turned_back, at - 1)
                    nc.vector.tensor_tensor_scan(scanned[:, slot % 2, :], stream[:, slot, :], ps[0:D, slot % 2, :],
                                                 0.0, ALU.mult, ALU.max).then_inc(scan_done, 1)
            walk_edges(dve, 3, edges1)

            dve.wait_ge(degree_moved, 16)
            nc.vector.tensor_scalar(degree[:, :], degree[:, :], 1.0, None, ALU.max).then_inc(degree_inverted, 1)
            dve.wait_ge(degree_inverted, 1)
            nc.vector.reciprocal(degree[:, :], degree[:, :]).then_inc(degree_inverted, 1)

            def outs(step):
                if (c := step.item(0)):
                    at, slot, turn = c
                    wait(dve, inverse_loaded[slot], (turn + 1) * 16)
                    wait(dve, e_out, at - 1)
                    nc.vector.tensor_tensor(mean_chunk[0:D, slot, :], sum_feat[0:D, bass.ds(at * CHUNK, CHUNK)],
                                            stream[:, slot, :], ALU.mult).then_inc(e_mean, 1)
                if (c := step.item(2)):
                    at, slot, turn = c
                    wait(dve, e_kept, at + 1)
                    hold(dve, dve_passed)
                    width = LAST if isinstance(at, int) and at == NCH - 1 else CHUNK
                    for k, kept in enumerate((sum_feat, max_feat)):
                        nc.vector.bn_stats(bn_stats[:, k, bass.ds(at, 1), :].rearrange("p a f -> p (a f)"),
                                           kept[0:D, bass.ds(at * CHUNK, width)]).then_inc(e_stats, 1)
            walk_nodes(dve, 2, outs)

            dve.wait_ge(e_stats, 2 * NCH)
            for k in range(2):
                nc.vector.bn_aggr(bn_mv[:, k, :], bn_stats[:, k, :, :]).then_inc(e_bn, 1)
            dve.wait_ge(e_bn, 2)
            dve.wait_ge(e_pow, 2)
            nc.vector.tensor_tensor(bn_a[:, :], bn_scale[:, :], bn_rstd[:, :], ALU.mult).then_inc(e_bn, 1)
            dve.wait_ge(e_bn, 3)
            nc.vector.tensor_tensor(bn_am[:, :], bn_a[:, :], bn_mv[:, :, 0], ALU.mult).then_inc(e_bn, 1)
            dve.wait_ge(e_bn, 4)
            nc.vector.tensor_tensor(bn_am[:, :], bn_shift[:, :], bn_am[:, :], ALU.subtract).then_inc(e_bn, 1)
            dve.wait_ge(e_bn, 5)
            nc.vector.tensor_tensor(bn_c[:, 2:3], bn_am[:, 0:1], bn_am[:, 1:2], ALU.add).then_inc(e_bn, 3)
            dve.wait_ge(e_kept, NCH)

            def finish(step):
                if (c := step.item(0)):
                    at, slot, turn = c
                    wait(dve, f_shift, at + 1)
                    nc.vector.scalar_tensor_tensor(out=shifted[:, slot, :],
                                                   in0=max_feat[:, bass.ds(at * CHUNK, CHUNK)], scalar=bn_a[:, 1:2],
                                                   in1=shifted[:, slot, :], op0=ALU.mult, op1=ALU.add)\
                      .then_inc(f_sum, 1)
                if (c := step.item(1)):
                    at, slot, turn = c
                    wait(dve, f_sum, at + 1)
                    wait(dve, f_turned, at - 1)
                    nc.vector.scalar_tensor_tensor(out=y_chunk[0:D, slot, :], in0=shifted[:, slot, :], scalar=0.01,
                                                   in1=shifted[:, slot, :], op0=ALU.mult, op1=ALU.max)\
                      .then_inc(f_leaky, 1)
                if (c := step.item(2)):
                    at, slot, turn = c
                    wait(dve, f_turned, at + 1)
                    wait(dve, f_stored[slot], turn * 16)
                    nc.vector.tensor_tensor(y_tile[:, slot, :, :],
                                            ps[:, 6 + slot, 0:4 * D].rearrange("p (t f) -> p t f", f=D),
                                            x_nodes[:, bass.ds(at * 4, 4), :], ALU.add).then_inc(f_added, 1)
            walk_nodes(dve, 2, finish)


_WEIGHTS = ["L0_gnn_mW1", "L0_gnn_mb1", "L0_gnn_mW2", "L0_gnn_mb2", "L0_gnn_gW1", "L0_gnn_gb1", "L0_gnn_gW2",
            "L0_gnn_gb2", "L0_gnn_uW1", "L0_gnn_ub1", "L0_gnn_uW2", "L0_gnn_ub2", "L0_gnn_ln_g", "L0_gnn_ln_b",
            "L1_gnn_W_self1", "L1_gnn_W_neigh1", "L1_gnn_W_pool", "L1_gnn_b_pool", "L1_gnn_W_self2",
            "L1_gnn_W_neigh2", "L1_gnn_g1", "L1_gnn_beta1", "L1_gnn_g2", "L1_gnn_beta2"]


def kernel(**inputs):
    import numpy as _np
    import concourse.bacc as _bacc
    from concourse import mybir as _mybir
    from concourse.bass_utils import run_bass_kernel_spmd as _run

    def lanes(v):
        return v.reshape(ET, P).T

    src = _np.pad(_np.asarray(inputs["src"]), (0, EPAD - E))
    dst = _np.pad(_np.asarray(inputs["dst"]), (1, EPAD - E + 1), constant_values=(-1, N))
    laid = {
        "x": _np.pad(_np.asarray(inputs["x"]), ((0, NPAD - N), (0, 0))).reshape(NT, P, D).transpose(1, 0, 2),
        "src_lanes": lanes(src),
        "dst_lanes": lanes(dst[1:EPAD + 1]),
        "dst_next_lanes": lanes(dst[2:EPAD + 2]),
        "dst_ext": dst[0:EPAD + 1],
        "edge_attr_t": _np.pad(_np.asarray(inputs["edge_attr_32"]), ((0, EPAD - E), (0, 0))).T,
    }
    for name in _WEIGHTS:
        laid[name] = _np.asarray(inputs[name])
    nc = _bacc.Bacc("TRN2", target_bir_lowering=False, num_devices=1)
    arrays, args = {}, []
    for name, a in laid.items():
        a = _np.ascontiguousarray(a)
        arrays[f"in_{name}"] = a
        args.append(nc.dram_tensor(f"in_{name}", a.shape, _mybir.dt.from_np(a.dtype), kind="ExternalInput").ap())
    args.append(nc.dram_tensor("out_0", (P, NT, D), _mybir.dt.float32, kind="ExternalOutput").ap())
    gnn(nc, *args)
    r = _run(nc, [arrays], core_ids=[0])
    return r.results[0]["out_0"].transpose(1, 0, 2).reshape(NPAD, D)[0:N]
```

```python
from contextlib import ExitStack

import concourse.bass as bass
from concourse import mybir

F32 = mybir.dt.float32
I32 = mybir.dt.int32
ALU = mybir.AluOpType
ACT = mybir.ActivationFunctionType

P = 128
N, E, D, DE = 6250, 106250, 96, 32
GROUP = 4
CHUNK = 4 * P
NCH = -(-N // CHUNK)
NPAD = NCH * CHUNK
NT = NPAD // P
LAST = N - (NCH - 1) * CHUNK
ET = -(-E // (P * GROUP)) * GROUP
EPAD = ET * P
NG = ET // GROUP
RING = 4
ROW0 = 2 * D
ROW1 = 2 * D + 1
BN_EPS = LN_EPS = 1e-5


class Step:

    def __init__(self, turn, slot, unroll, count):
        self.turn, self.slot, self.unroll, self.count = turn, slot, unroll, count

    def item(self, lag=0):
        slot, turn = self.slot - lag, self.turn
        while slot < 0:
            slot, turn = slot + self.unroll, turn - 1
        at = turn * self.unroll + slot
        if isinstance(at, int) and not 0 <= at < self.count:
            return None
        return at, slot, turn


def walk(engine, count, lags, unroll, peeled, body):
    for s in range(peeled):
        body(Step(s // unroll, s % unroll, unroll, count))
    with engine.Fori(peeled // unroll, count // unroll) as turn:
        for k in range(unroll):
            body(Step(turn, k, unroll, count))
    for s in range(count // unroll * unroll, count + lags):
        body(Step(s // unroll, s % unroll, unroll, count))


def walk_edges(engine, lags, body):
    walk(engine, NG, lags, RING, 2 * RING, body)


def walk_nodes(engine, lags, body):
    walk(engine, NCH, lags, 2, 6, body)


def wait(engine, sem, value):
    if not isinstance(value, int) or value > 0:
        engine.wait_ge(sem, value)


def hold(engine, passed):
    engine.sem_inc(passed, 1)


def gnn(nc, x, src_lanes, dst_lanes, dst_next_lanes, dst_ext, edge_attr_t,
        mW1, mb1, mW2, mb2, gW1, gb1, gW2, gb2, uW1, ub1, uW2, ub2, ln_g, ln_b,
        W_self1, W_neigh1, W_pool, b_pool, W_self2, W_neigh2, g1, beta1, g2, beta2, out):
    with ExitStack() as ctx:
        def sb(name, shape, dt=F32):
            return ctx.enter_context(nc.sbuf_tensor(name, shape, dt))

        def sem(name):
            return ctx.enter_context(nc.semaphore(name))

        def sems(name, n):
            return [sem(f"{name}{i}") for i in range(n)]

        table0 = nc.dram_tensor("table0", (NPAD, ROW0), F32)
        table1 = nc.dram_tensor("table1", (NPAD, ROW1), F32)
        same_dst = nc.dram_tensor("same_dst", (EPAD,), F32)
        inv_degree = nc.dram_tensor("inv_degree", (NPAD,), F32)

        x_nodes = sb("x_nodes", [P, NT, D])
        self_feat = sb("self_feat", [P, NPAD])
        h_nodes = self_feat[:, 0:NT * D].rearrange("p (t f) -> p t f", f=D)
        h_feat = sb("h_feat", [D + 1, NPAD])
        sum_feat = sb("sum_feat", [D + 1, NPAD])
        max_feat = sb("max_feat", [D, NPAD])

        rows = sb("rows", [P, RING, GROUP * ROW1])
        indices = sb("indices", [P, RING, GROUP], I32)
        stream = sb("stream", [P, RING, CHUNK])
        pre = sb("pre", [P, 2, GROUP * ROW0])
        gate_act = sb("gate_act", [P, 2, GROUP, D])
        msg = sb("msg", [P, 2, GROUP, D + 1])
        logit = sb("logit", [P, 2, GROUP])
        tanh = sb("tanh", [P, 2, GROUP])
        gate = sb("gate", [P, 2, GROUP])
        onehot = sb("onehot", [P, RING, GROUP, P])
        scanned = sb("scanned", [D, 2, GROUP * P])
        ends = sb("ends", [P, 2, GROUP, D])

        h_tile = sb("h_tile", [P, 2, 4, D])
        h_chunk = sb("h_chunk", [D + 1, 2, CHUNK])
        u_chunk = sb("u_chunk", [D + 1, 2, CHUNK])
        y_tile = sb("y_tile", [P, 2, 4, D])
        out_rows = rows
        mean_chunk, scaled1, summed_parts = u_chunk, u_chunk, h_chunk
        stats = sb("stats", [P, 2, 4, 6])
        mv = sb("mv", [P, 2, 4, 2])
        rstd = sb("rstd", [P, 2, 4])
        nmr = sb("nmr", [P, 2, 4])
        mv2 = sb("mv2", [P, 2, 4, 2])
        rstd2 = sb("rstd2", [P, 2, 4])
        nmr2 = sb("nmr2", [P, 2, 4])
        var_eps = sb("var_eps", [P, 4])
        var_eps2 = sb("var_eps2", [P, 4])
        power = sb("power", [P, 4])
        degree = sb("degree", [P, NT])

        dst_i = sb("dst_i", [P, ET], I32)
        dst_rel = sb("dst_rel", [P, ET])
        is_end = sb("is_end", [P, ET])

        ident = sb("ident", [P, P])
        columns = sb("columns", [P, P])
        lane = sb("lane", [P, 1])
        ones = sb("ones", [P, P])
        w_table0 = sb("w_table0", [D + 1, ROW0])
        w_edge = sb("w_edge", [P, GROUP, ROW0])
        w_gate = sb("w_gate", [P, D])
        b_gate = sb("b_gate", [P, 1])
        w_m2 = sb("w_m2", [D, D])
        w_m2t = sb("w_m2t", [D, D + 1])
        w_u1_agg = sb("w_u1_agg", [D, D])
        w_u1_h = sb("w_u1_h", [D + 1, D])
        w_u1_sum = sb("w_u1_sum", [D + 1, D])
        w_u2 = sb("w_u2", [D + 1, D])
        scale_ln = sb("scale_ln", [P, D])
        shift_ln = sb("shift_ln", [P, D])
        w_pool = sb("w_pool", [D + 1, D])
        w_self = sb("w_self", [D, 2, D])
        w_neigh = sb("w_neigh", [D, 2, D])
        bn_scale = sb("bn_scale", [D, 2])
        bn_shift = sb("bn_shift", [D, 2])
        bn_stats = sb("bn_stats", [D, 2, NCH, 6])
        bn_mv = sb("bn_mv", [D, 2, 2])
        bn_rstd = sb("bn_rstd", [D, 2])
        bn_a = sb("bn_a", [D, 2])
        bn_am = sb("bn_am", [D, 2])
        bn_c = sb("bn_c", [D, 3])

        ps = ctx.enter_context(nc.psum_tensor("ps", [P, 8, 512], F32))

        edges_loaded = sem("edges_loaded")
        pool_passed = sem("pool_passed")
        dve_passed = sem("dve_passed")
        table_weights_loaded = sem("table_weights_loaded")
        edge_weights_loaded = sem("edge_weights_loaded")
        node_weights_loaded = sem("node_weights_loaded")
        x_loaded = sems("x_loaded", 4)
        consts_made = sem("consts_made")
        columns_made = sem("columns_made")
        cleared = sem("cleared")
        biases_made = sem("biases_made")
        same_made = sem("same_made")
        same_stored = sem("same_stored")
        dst_float = sem("dst_float")
        base_spread = sem("base_spread")
        dst_ready = sem("dst_ready")
        sums_zero = sem("sums_zero")
        maxima_zero = sem("maxima_zero")
        ones_made = sem("ones_made")
        edge_weights_zero = sem("edge_weights_zero")
        m2_turned = sem("m2_turned")
        m2_copied = sem("m2_copied")
        u1_product = sem("u1_product")
        u1_ready = sem("u1_ready")
        prep_bn_stats = sem("prep_bn_stats")
        prep_stats = sem("prep_stats")
        prep_eps = sem("prep_eps")
        prep_rstd = sem("prep_rstd")
        prep_nmr = sem("prep_nmr")
        prep_h = sem("prep_h")
        prep_turned = sem("prep_turned")
        prep_copied = sem("prep_copied")
        prep_kept = sem("prep_kept")
        prep_shifted = sem("prep_shifted")
        prep_product = sem("prep_product")
        prep_evac = sem("prep_evac")
        prep_stored = sems("prep_stored", 2)
        attr_loaded = sems("attr_loaded", RING)
        index_loaded = sems("index_loaded", RING)
        gathered = sems("gathered", RING)
        pre_product = sem("pre_product")
        pre_added = sem("pre_added")
        gate_gelu = sem("gate_gelu")
        msg_gelu = sem("msg_gelu")
        logits_done = sem("logits_done")
        tanh_done = sem("tanh_done")
        gate_done = sem("gate_done")
        onehot_done = sem("onehot_done")
        summed = sem("summed")
        window_added = sem("window_added")
        update_hidden = sem("update_hidden")
        update_gelu = sem("update_gelu")
        update_product = sem("update_product")
        update_residual = sem("update_residual")
        update_bn_stats = sem("update_bn_stats")
        update_stats = sem("update_stats")
        update_eps = sem("update_eps")
        update_rstd = sem("update_rstd")
        update_scaled = sem("update_scaled")
        update_x_added = sem("update_x_added")
        update_bn_stats2 = sem("update_bn_stats2")
        update_stats2 = sem("update_stats2")
        update_eps2 = sem("update_eps2")
        update_rstd2 = sem("update_rstd2")
        update_nmr = sem("update_nmr")
        update_normalized = sem("update_normalized")
        update_nmr2 = sem("update_nmr2")
        update_h_rows = sem("update_h_rows")
        update_turned = sem("update_turned")
        update_copied = sem("update_copied")
        update_kept = sem("update_kept")
        update_pooled = sem("update_pooled")
        update_evac = sem("update_evac")
        update_stored = sems("update_stored", RING)
        self_product = sem("self_product")
        self_kept = sem("self_kept")
        mask_loaded = sems("mask_loaded", RING)
        index1_loaded = sems("index1_loaded", RING)
        gathered1 = sems("gathered1", RING)
        sums_cleared = sem("sums_cleared")
        turned = sem("turned")
        scan_done = sem("scan_done")
        onehot1_done = sem("onehot1_done")
        turned_back = sem("turned_back")
        ends_done = sem("ends_done")
        picked = sem("picked")
        rows_summed = sem("rows_summed")
        sums_added = sem("sums_added")
        maxima_added = sem("maxima_added")
        degree_moved = sem("degree_moved")
        degree_inverted = sem("degree_inverted")
        inverse_stored = sem("inverse_stored")
        inverse_loaded = sems("inverse_loaded", 2)
        out_mean = sem("out_mean")
        out_products = sem("out_products")
        out_stats = sem("out_stats")
        out_kept = sem("out_kept")
        out2_kept = sem("out2_kept")
        norm_coefficients = sem("norm_coefficients")
        norm_rstd = sem("norm_rstd")
        finish_scaled1 = sem("finish_scaled1")
        finish_summed = sem("finish_summed")
        finish_evac = sem("finish_evac")
        finish_leaky = sem("finish_leaky")
        finish_turned = sem("finish_turned")
        finish_added = sem("finish_added")
        finish_stored = sems("finish_stored", 2)

        block = ctx.enter_context(nc.Block())

        staging = rows[:, :, :].rearrange("p a b -> p (a b)").bitcast(I32)
        row_dst = staging[:, 0:ET]
        row_prev = staging[:, ET:2 * ET]
        next_i = is_end[:, :].bitcast(I32)
        same = onehot[:, :, :, :].rearrange("p a b c -> p (a b c)")[:, 0:ET]
        N_EDGE_LOADS = 4
        N_TABLE_WEIGHTS, N_EDGE_WEIGHTS, N_NODE_WEIGHTS = 5, 5 + 2 * GROUP, 15
        X_PIECES = ((0, 1), (1, 4), (4, 8), (8, NCH))

        def as_row(v):
            return v.rearrange("(a n) -> a n", a=1)

        def as_column(v):
            return v.rearrange("(n a) -> n a", a=1)

        def rows0(slot):
            return rows[:, slot, 0:GROUP * ROW0]

        def tile_rows(t):
            return t.rearrange("(t p) f -> p t f", p=P)

        @block.sync
        def _(sp):
            def load_x(k):
                first, end = X_PIECES[k]
                sp.dma_start(x_nodes[:, first * 4:end * 4, :], x[:, first * 4:end * 4, :]).then_inc(x_loaded[k], 16)

            load_x(0)
            load_x(1)
            sp.wait_ge(edge_weights_zero, 1)
            for j in range(GROUP):
                for k, w in enumerate((mW1, gW1)):
                    sp.dma_start(w_edge[j * DE:(j + 1) * DE, j, k * D:(k + 1) * D], w[D:D + DE, :])\
                      .then_inc(edge_weights_loaded, 16)
            for to, of in ((w_gate[:, :], gW2.rearrange("n a -> (n a)").partition_broadcast(P)),
                           (b_gate[:, :], gb2.partition_broadcast(P)), (w_m2[:, :], mW2),
                           (w_m2t[:, D:D + 1], as_column(mb2)), (w_u1_agg[:, :], uW1[D:2 * D, :])):
                sp.dma_start(to, of).then_inc(edge_weights_loaded, 16)
            load_x(2)
            load_x(3)
            sp.dma_start(row_dst, dst_ext[1:EPAD + 1].rearrange("(p t) -> p t", p=P)).then_inc(edges_loaded, 16)
            sp.dma_start(row_prev, dst_ext[0:EPAD].rearrange("(p t) -> p t", p=P)).then_inc(edges_loaded, 16)
            sp.dma_start(dst_i[:, :], dst_lanes).then_inc(edges_loaded, 16)
            sp.dma_start(next_i, dst_next_lanes).then_inc(edges_loaded, 16)

            def store0(step):
                if (c := step.item(3)):
                    at, slot, turn = c
                    wait(sp, prep_evac, at + 1)
                    sp.dma_start(tile_rows(table0)[:, bass.ds(at * 4, 4), :],
                                 pre[:, slot, :].rearrange("p (t f) -> p t f", f=ROW0)).then_inc(prep_stored[slot], 16)
            walk_nodes(sp, 3, store0)

            sp.wait_ge(same_made, 1)
            sp.dma_start(same_dst.rearrange("(p t) -> p t", p=P), same).then_inc(same_stored, 16)

            def load0(step):
                at, slot, turn = step.item()
                wait(sp, gathered[slot], turn * 64)
                sp.dma_start(indices[:, slot, :], src_lanes[:, bass.ds(at * GROUP, GROUP)])\
                  .then_inc(index_loaded[slot], 16)
                wait(sp, pre_product, at - RING + 1)
                sp.dma_start(stream[:, slot, 0:P], edge_attr_t[:, bass.ds(at * P, P)])\
                  .then_inc(attr_loaded[slot], 16)
            walk_edges(sp, 0, load0)

            for to, of in ((w_u1_h[0:D, :], uW1[0:D, :]), (w_u1_h[D:D + 1, :], as_row(ub1)),
                           (w_u2[0:D, :], uW2), (w_u2[D:D + 1, :], as_row(ub2)),
                           (scale_ln[:, :], ln_g.partition_broadcast(P)),
                           (w_pool[0:D, :], W_pool), (w_pool[D:D + 1, :], as_row(b_pool))):
                sp.dma_start(to, of).then_inc(node_weights_loaded, 16)
            for k, (w_s, w_n, g, b) in enumerate(((W_self1, W_neigh1, g1, beta1), (W_self2, W_neigh2, g2, beta2))):
                for to, of in ((w_self[:, k, :], w_s), (w_neigh[:, k, :], w_n), (bn_scale[:, k:k + 1], as_column(g)),
                               (bn_shift[:, k:k + 1], as_column(b))):
                    sp.dma_start(to, of).then_inc(node_weights_loaded, 16)

            def store1(step):
                if (c := step.item(5)):
                    at, slot, turn = c
                    wait(sp, update_evac, at + 1)
                    sp.dma_start(tile_rows(table1)[:, bass.ds(at * 4, 4), :],
                                 out_rows[:, slot, :].rearrange("p (t f) -> p t f", f=ROW1))\
                      .then_inc(update_stored[slot], 16)
            walk(sp, NCH, 5, RING, 2 * RING, store1)

            sp.wait_ge(same_stored, 16)
            sp.wait_ge(pre_product, NG)
            for slot in range(RING):
                sp.wait_ge(gathered[slot], 64 * (NG // RING))

            def load1(step):
                at, slot, turn = step.item()
                wait(sp, gathered1[slot], turn * 64)
                sp.dma_start(indices[:, slot, :], src_lanes[:, bass.ds(at * GROUP, GROUP)])\
                  .then_inc(index1_loaded[slot], 16)
                wait(sp, scan_done, at - RING + 1)
                sp.dma_start(stream[0:D, slot, :],
                             same_dst[bass.ds(at * CHUNK, CHUNK)].partition_broadcast(D))\
                  .then_inc(mask_loaded[slot], 16)
            walk_edges(sp, 0, load1)

            sp.wait_ge(sums_added, ET)
            sp.dma_start(degree[:, :], sum_feat[D:D + 1, :].rearrange("a (p t) -> a p t", p=P)).then_inc(degree_moved, 16)
            sp.wait_ge(degree_inverted, 2)
            sp.dma_start(inv_degree.rearrange("(p t) -> p t", p=P), degree[:, :]).then_inc(inverse_stored, 16)
            sp.wait_ge(inverse_stored, 16)

            def load_inverse(step):
                at, slot, turn = step.item()
                wait(sp, out_mean, at - 1)
                sp.dma_start(stream[0:D, slot, :],
                             inv_degree[bass.ds(at * CHUNK, CHUNK)].partition_broadcast(D))\
                  .then_inc(inverse_loaded[slot], 16)
            walk_nodes(sp, 0, load_inverse)

            def store_out(step):
                if (c := step.item(3)):
                    at, slot, turn = c
                    wait(sp, finish_added, at + 1)
                    sp.dma_start(out[:, bass.ds(at * 4, 4), :], x_nodes[:, bass.ds(at * 4, 4), :])\
                      .then_inc(finish_stored[slot], 16)
            walk_nodes(sp, 3, store_out)
            sp.wait_ge(finish_stored[0], 16 * ((NCH + 1) // 2))
            sp.wait_ge(finish_stored[1], 16 * (NCH // 2))


        @block.gpsimd
        def _(pool):
            nc.gpsimd.memset(power[:, :], -0.5).then_inc(consts_made, 1)
            nc.gpsimd.memset(ident[:, :], 0.0).then_inc(consts_made, 1)
            nc.gpsimd.memset(ones[:, :], 1.0).then_inc(consts_made, 1)
            pool.wait_ge(consts_made, 3)
            nc.gpsimd.affine_select(out=ident[:, :], in_=ident[:, :], compare_op=ALU.not_equal, fill=1.0,
                                    base=0, pattern=[[-1, P]], channel_multiplier=1).then_inc(consts_made, 1)
            nc.gpsimd.iota(columns[:, :], [[1, P]], 0, 0, allow_small_or_imprecise_dtypes=True)\
              .then_inc(columns_made, 1)
            nc.gpsimd.iota(lane[:, :], [[0, 1]], 0, 1, allow_small_or_imprecise_dtypes=True)\
              .then_inc(columns_made, 1)
            pool.wait_ge(columns_made, 2)

            def prepare(step):
                if (c := step.item(0)):
                    at, slot, turn = c
                    wait(pool, prep_stats, at + 1)
                    wait(pool, prep_rstd, at)
                    hold(pool, pool_passed)
                    nc.gpsimd.tensor_scalar(var_eps[:, :], mv[:, slot, :, 1], LN_EPS, None, ALU.add)\
                      .then_inc(prep_eps, 1)
                    wait(pool, prep_eps, at + 1)
                    wait(pool, prep_nmr, at - 1)
                    wait(pool, prep_h, at - 1)
                    nc.gpsimd.tensor_tensor(rstd[:, slot, :], var_eps[:, :], power[:, :], ALU.pow)\
                      .then_inc(prep_rstd, 1)
                if (c := step.item(2)):
                    at, slot, turn = c
                    wait(pool, prep_h, at + 1)
                    if isinstance(at, int) and at == 0:
                        pool.wait_ge(table_weights_loaded, 16 * N_TABLE_WEIGHTS)
                    hold(pool, pool_passed)
                    chunk = x_nodes[:, bass.ds(at * 4, 4), :]
                    nc.gpsimd.tensor_tensor(chunk, chunk, shift_ln[:, :].unsqueeze(1).to_broadcast([P, 4, D]), ALU.add)\
                      .then_inc(prep_shifted, 1)
            walk_nodes(pool, 2, prepare)
            pool.wait_ge(prep_shifted, NCH)
            nc.gpsimd.memset(h_feat[D:D + 1, :], 1.0).then_inc(biases_made, 1)

            pool.wait_ge(prep_stored[0], 16 * ((NCH + 1) // 2))
            pool.wait_ge(prep_stored[1], 16 * (NCH // 2))
            pool.wait_ge(same_made, 1)

            def gather0(step):
                at, slot, turn = step.item()
                wait(pool, index_loaded[slot], (turn + 1) * 16)
                wait(pool, pre_added, at - RING + 1)
                hold(pool, pool_passed)
                for j in range(GROUP):
                    nc.gpsimd.indirect_dma_start(
                        rows[:, slot, j * ROW0:(j + 1) * ROW0], None, table0[:, :],
                        bass.IndirectOffsetOnAxis(ap=indices[:, slot, j:j + 1], axis=0)).then_inc(gathered[slot], 16)
            walk_edges(pool, 0, gather0)

            def update(step):
                if (c := step.item(3)):
                    at, slot, turn = c
                    wait(pool, update_stats2, at + 1)
                    wait(pool, update_rstd2, at)
                    hold(pool, pool_passed)
                    nc.gpsimd.tensor_scalar(var_eps2[:, :], mv2[:, slot % 2, :, 1], LN_EPS, None, ALU.add)\
                      .then_inc(update_eps2, 1)
                    wait(pool, update_eps2, at + 1)
                    wait(pool, update_h_rows, at - 1)
                    nc.gpsimd.tensor_tensor(rstd2[:, slot % 2, :], var_eps2[:, :], power[:, :], ALU.pow)\
                      .then_inc(update_rstd2, 1)
                if (c := step.item(2)):
                    at, slot, turn = c
                    wait(pool, update_normalized, at + 1)
                    hold(pool, pool_passed)
                    y = y_tile[:, slot % 2, :, :]
                    nc.gpsimd.tensor_tensor(y, y, scale_ln[:, :].unsqueeze(1).to_broadcast([P, 4, D]), ALU.mult)\
                      .then_inc(update_scaled, 1)
                if (c := step.item(1)):
                    at, slot, turn = c
                    wait(pool, update_stats, at + 1)
                    wait(pool, update_rstd, at)
                    hold(pool, pool_passed)
                    nc.gpsimd.tensor_scalar(var_eps[:, :], mv[:, slot % 2, :, 1], LN_EPS, None, ALU.add)\
                      .then_inc(update_eps, 1)
                    wait(pool, update_eps, at + 1)
                    wait(pool, update_normalized, at - 1)
                    nc.gpsimd.tensor_tensor(rstd[:, slot % 2, :], var_eps[:, :], power[:, :], ALU.pow)\
                      .then_inc(update_rstd, 1)
            walk(pool, NCH, 5, RING, 2 * RING, update)

            for slot in range(RING):
                pool.wait_ge(update_stored[slot], 16 * -(-(NCH - slot) // RING))

            def gather1(step):
                at, slot, turn = step.item()
                wait(pool, index1_loaded[slot], (turn + 1) * 16)
                wait(pool, rows_summed, at - RING + 1)
                hold(pool, pool_passed)
                for j in range(GROUP):
                    nc.gpsimd.indirect_dma_start(
                        rows[:, slot, j * ROW1:(j + 1) * ROW1], None, table1[:, :],
                        bass.IndirectOffsetOnAxis(ap=indices[:, slot, j:j + 1], axis=0)).then_inc(gathered1[slot], 16)
            walk_edges(pool, 0, gather1)

            pool.wait_ge(norm_coefficients, 2)
            nc.gpsimd.tensor_scalar(bn_c[:, 0:2], bn_mv[:, :, 1], BN_EPS, None, ALU.add).then_inc(norm_rstd, 1)
            pool.wait_ge(norm_rstd, 1)
            nc.gpsimd.tensor_tensor(bn_rstd[:, :], bn_c[:, 0:2], power[0:D, 0:2], ALU.pow).then_inc(norm_rstd, 1)

            def finish(step):
                if (c := step.item(3)):
                    at, slot, turn = c
                    wait(pool, finish_leaky, at + 1)
                    chunk = x_nodes[:, bass.ds(at * 4, 4), :]
                    nc.gpsimd.tensor_tensor(chunk, chunk, y_tile[:, slot, :, :], ALU.add).then_inc(finish_added, 1)
            walk_nodes(pool, 3, finish)

        @block.scalar
        def _(act):
            for to, of in ((w_table0[0:D, 0:D], mW1[0:D, :]), (w_table0[0:D, D:ROW0], gW1[0:D, :]),
                           (w_table0[D:D + 1, 0:D], as_row(mb1)), (w_table0[D:D + 1, D:ROW0], as_row(gb1)),
                           (shift_ln[:, :], ln_b.partition_broadcast(P))):
                act.dma_start(to, of).then_inc(table_weights_loaded, 16)

            def prepare(step):
                if (c := step.item(1)):
                    at, slot, turn = c
                    wait(act, prep_nmr, at + 1)
                    wait(act, prep_turned, at - 1)
                    wait(act, prep_kept, 2 * (at - 1))
                    for j in range(4):
                        last = nc.scalar.activation(h_tile[:, slot, j, :], x_nodes[:, bass.ds(at * 4 + j, 1), :]
                                                    .rearrange("p a f -> p (a f)"), ACT.Relu,
                                                    bias=nmr[:, slot, j:j + 1], scale=rstd[:, slot, j:j + 1])
                    last.then_inc(prep_h, 1)
                if (c := step.item(3)):
                    at, slot, turn = c
                    wait(act, prep_product, at + 1)
                    wait(act, prep_stored[slot], turn * 16)
                    nc.scalar.activation(pre[:, slot, :].rearrange("p (b f) -> p b f", b=2),
                                         ps[:, 2 + 2 * slot:4 + 2 * slot, 0:2 * ROW0], ACT.Copy).then_inc(prep_evac, 1)
            walk_nodes(act, 3, prepare)

            act.wait_ge(prep_stored[0], 16 * ((NCH + 1) // 2))
            act.wait_ge(prep_stored[1], 16 * (NCH // 2))

            def edges0(step):
                if (c := step.item(1)):
                    at, slot, turn = c
                    wait(act, logits_done, at + 1)
                    wait(act, gate_done, at - 1)
                    nc.scalar.activation(tanh[:, slot % 2, :], logit[:, slot % 2, :], ACT.Tanh,
                                         bias=b_gate[:, 0:1], scale=0.5).then_inc(tanh_done, 1)
                if (c := step.item(0)):
                    at, slot, turn = c
                    z = pre[:, slot % 2, :].rearrange("p (t k f) -> p t k f", t=GROUP, k=2)
                    wait(act, pre_added, at + 1)
                    wait(act, logits_done, at - 1)
                    nc.scalar.activation(gate_act[:, slot % 2, :, :], z[:, :, 1, :], ACT.Gelu).then_inc(gate_gelu, 1)
                    wait(act, summed, at - 1)
                    nc.scalar.activation(msg[:, slot % 2, :, 0:D], z[:, :, 0, :], ACT.Gelu).then_inc(msg_gelu, 1)
            act.wait_ge(u1_ready, 1)
            walk_edges(act, 1, edges0)

            act.wait_ge(ones_made, GROUP)

            def update(step):
                if (c := step.item(2)):
                    at, slot, turn = c
                    wait(act, update_nmr, at + 1)
                    wait(act, update_x_added, at - 1)
                    for j in range(4):
                        last = nc.scalar.activation(y_tile[:, slot % 2, j, :], h_tile[:, slot % 2, j, :], ACT.Identity,
                                                    bias=nmr[:, slot % 2, j:j + 1], scale=rstd[:, slot % 2, j:j + 1])
                    last.then_inc(update_normalized, 1)
                if (c := step.item(0)):
                    at, slot, turn = c
                    wait(act, update_hidden, at + 1)
                    wait(act, update_product, at - 1)
                    nc.scalar.activation(u_chunk[0:D, slot % 2, :], ps[0:D, slot % 2, :], ACT.Gelu).then_inc(update_gelu, 1)
                if (c := step.item(4)):
                    at, slot, turn = c
                    wait(act, update_nmr2, at + 1)
                    wait(act, update_stored[slot], turn * 16)
                    for j in range(4):
                        last = nc.scalar.activation(out_rows[:, slot, j * ROW1:j * ROW1 + D],
                                                    x_nodes[:, bass.ds(at * 4 + j, 1), :]
                                                    .rearrange("p a f -> p (a f)"), ACT.Relu,
                                                    bias=nmr2[:, slot % 2, j:j + 1], scale=rstd2[:, slot % 2, j:j + 1])
                    last.then_inc(update_h_rows, 1)
                if (c := step.item(5)):
                    at, slot, turn = c
                    wait(act, update_copied, at + 1)
                    nc.scalar.activation(h_feat[0:D, bass.ds(at * CHUNK, CHUNK)], ps[0:D, 4 + slot % 2, :], ACT.Copy)\
                      .then_inc(update_kept, 1)
                if (c := step.item(5)):
                    at, slot, turn = c
                    wait(act, update_pooled, at + 1)
                    nc.scalar.activation(out_rows[:, slot, :].rearrange("p (t f) -> p t f", f=ROW1)[:, :, D + 1:ROW1],
                                         ps[:, 6 + slot % 2, 0:4 * D].rearrange("p (t f) -> p t f", f=D), ACT.Relu)\
                      .then_inc(update_evac, 1)
            walk(act, NCH, 5, RING, 2 * RING, update)

            def self_part(step):
                at, slot, turn = step.item()
                wait(act, self_product, at + 1)
                nc.scalar.activation(self_feat[0:D, bass.ds(at * CHUNK, CHUNK)], ps[0:D, slot, :], ACT.Copy)\
                  .then_inc(self_kept, 1)
            walk_nodes(act, 0, self_part)

            def edges1(step):
                if (c := step.item(1)):
                    at, slot, turn = c
                    wait(act, turned_back, at + 1)
                    wait(act, picked, at - 1)
                    for j in range(GROUP):
                        last = nc.scalar.activation(ends[:, slot % 2, j, :], ps[:, 2 + slot % 2, j * D:(j + 1) * D],
                                                    ACT.Copy, scale=is_end[:, bass.ds(at * GROUP + j, 1)])
                    last.then_inc(ends_done, 1)
            walk_edges(act, 1, edges1)

            def outs(step):
                if (c := step.item(2)):
                    at, slot, turn = c
                    wait(act, out_products, at + 1)
                    nc.scalar.activation(sum_feat[0:D, bass.ds(at * CHUNK, CHUNK)], ps[0:D, 2 + slot, :], ACT.Copy)\
                      .then_inc(out_kept, 1)
            walk_nodes(act, 2, outs)

            act.wait_ge(norm_coefficients, 6)

            def finish(step):
                if (c := step.item(0)):
                    at, slot, turn = c
                    wait(act, finish_summed, at - 1)
                    nc.scalar.activation(scaled1[0:D, slot, :], sum_feat[0:D, bass.ds(at * CHUNK, CHUNK)],
                                         ACT.Identity, bias=bn_c[:, 2:3], scale=bn_a[:, 0:1]).then_inc(finish_scaled1, 1)
                if (c := step.item(2)):
                    at, slot, turn = c
                    wait(act, finish_turned, at + 1)
                    wait(act, finish_added, at - 1)
                    nc.scalar.activation(y_tile[:, slot, :, :].rearrange("p t f -> p (t f)"), ps[:, 6 + slot, 0:4 * D],
                                         ACT.Copy).then_inc(finish_evac, 1)
            walk_nodes(act, 2, finish)

        @block.tensor
        def _(pe):
            pe.wait_ge(consts_made, 4)
            pe.wait_ge(table_weights_loaded, 16 * N_TABLE_WEIGHTS)
            pe.wait_ge(cleared, 2)

            def prepare(step):
                if (c := step.item(1)):
                    at, slot, turn = c
                    wait(pe, prep_h, at + 1)
                    wait(pe, prep_copied, at - 1)
                    for j in range(4):
                        last = nc.tensor.transpose(ps[0:D, slot, j * P:(j + 1) * P], h_tile[:, slot, j, :], ident[:, :])
                    last.then_inc(prep_turned, 1)
                if (c := step.item(2)):
                    at, slot, turn = c
                    wait(pe, prep_copied, at + 1)
                    wait(pe, prep_evac, at - 1)
                    for j in range(4):
                        last = nc.tensor.matmul(ps[:, 2 + 2 * slot + j // 2, (j % 2) * ROW0:(j % 2 + 1) * ROW0],
                                                h_chunk[:, slot, j * P:(j + 1) * P], w_table0[:, :],
                                                start=True, stop=True)
                    last.then_inc(prep_product, 1)
            walk_nodes(pe, 2, prepare)

            pe.wait_ge(dst_float, 1)
            half = ET // 2
            for k in range(2):
                last = nc.tensor.matmul(ps[:, 6 + k, 0:half], ones[0:1, :], dst_rel[0:1, k * half:(k + 1) * half],
                                        start=True, stop=True)
            last.then_inc(base_spread, 1)

            pe.wait_ge(dst_ready, 3)
            pe.wait_ge(edge_weights_loaded, 16 * N_EDGE_WEIGHTS)
            nc.tensor.transpose(ps[0:D, 6, 0:D], w_m2[:, :], ident[0:D, 0:D]).then_inc(m2_turned, 1)
            pe.wait_ge(m2_copied, 1)
            nc.tensor.matmul(ps[0:D + 1, 7, 0:D], w_m2t[:, :], w_u1_agg[:, :], start=True, stop=True)\
              .then_inc(u1_product, 1)

            pe.wait_ge(prep_evac, NCH)
            pe.wait_ge(prep_copied, NCH)

            def edges0(step):
                if (c := step.item(0)):
                    at, slot, turn = c
                    wait(pe, attr_loaded[slot], (turn + 1) * 16)
                    wait(pe, pre_added, at - 1)
                    for j in range(GROUP // 2):
                        last = nc.tensor.matmul(
                            ps[:, 2 * (slot % 2) + j, 0:2 * ROW0], stream[:, slot, 0:P],
                            w_edge[:, 2 * j:2 * j + 2, :].rearrange("p t f -> p (t f)"), start=True, stop=True)
                    last.then_inc(pre_product, 1)
                if (c := step.item(2)):
                    at, slot, turn = c
                    wait(pe, msg_gelu, at + 1)
                    wait(pe, onehot_done, at + 1)
                    wait(pe, window_added, 4 * (at - 1))
                    for j in range(GROUP):
                        last = nc.tensor.matmul(ps[0:D + 1, 4 + slot % 2, j * P:(j + 1) * P], msg[:, slot % 2, j, :],
                                                onehot[:, slot % 2, j, :], start=True, stop=True)
                    last.then_inc(summed, 1)
            walk_edges(pe, 2, edges0)

            pe.wait_ge(pre_added, NG)
            pe.wait_ge(u1_ready, 2)
            pe.wait_ge(node_weights_loaded, 16 * N_NODE_WEIGHTS)
            pe.wait_ge(prep_kept, 2 * NCH)
            pe.wait_ge(biases_made, 1)

            def update(step):
                if (c := step.item(0)):
                    at, slot, turn = c
                    wait(pe, update_gelu, at - 1)
                    nc.tensor.matmul(ps[0:D, slot % 2, :], w_u1_h[:, :], h_feat[:, bass.ds(at * CHUNK, CHUNK)],
                                     start=True, stop=False)
                    if isinstance(at, int) and at == 0:
                        pe.wait_ge(window_added, ET)
                    nc.tensor.matmul(ps[0:D, slot % 2, :], w_u1_sum[:, :], sum_feat[:, bass.ds(at * CHUNK, CHUNK)],
                                     start=False, stop=True).then_inc(update_hidden, 1)
                if (c := step.item(5)):
                    at, slot, turn = c
                    wait(pe, update_h_rows, at + 1)
                    wait(pe, update_copied, at - 1)
                    wait(pe, update_kept, at - 1)
                    for j in range(4):
                        last = nc.tensor.transpose(ps[0:D, 4 + slot % 2, j * P:(j + 1) * P],
                                                   out_rows[:, slot, j * ROW1:j * ROW1 + D], ident[:, :])
                    last.then_inc(update_turned, 1)
                if (c := step.item(1)):
                    at, slot, turn = c
                    wait(pe, update_gelu, at + 1)
                    wait(pe, update_residual, at - 1)
                    for j in range(4):
                        last = nc.tensor.matmul(ps[:, 2 + slot % 2, j * D:(j + 1) * D], u_chunk[:, slot % 2, j * P:(j + 1) * P],
                                                w_u2[:, :], start=True, stop=True)
                    last.then_inc(update_product, 1)
                if (c := step.item(5)):
                    at, slot, turn = c
                    wait(pe, update_copied, at + 1)
                    wait(pe, update_evac, at - 1)
                    for j in range(4):
                        last = nc.tensor.matmul(ps[:, 6 + slot % 2, j * D:(j + 1) * D], h_chunk[:, slot % 2, j * P:(j + 1) * P],
                                                w_pool[:, :], start=True, stop=True)
                    last.then_inc(update_pooled, 1)
            walk(pe, NCH, 5, RING, 2 * RING, update)

            pe.wait_ge(update_evac, NCH)
            pe.wait_ge(update_copied, NCH)
            pe.wait_ge(update_residual, NCH)

            def self_part(step):
                at, slot, turn = step.item()
                wait(pe, self_kept, at - 1)
                nc.tensor.matmul(ps[0:D, slot, :], w_self[:, 1, :], h_feat[0:D, bass.ds(at * CHUNK, CHUNK)],
                                 start=True, stop=True).then_inc(self_product, 1)
            walk_nodes(pe, 0, self_part)
            pe.wait_ge(self_kept, NCH)

            def edges1(step):
                if (c := step.item(2)):
                    at, slot, turn = c
                    wait(pe, ends_done, at + 1)
                    wait(pe, maxima_added, GROUP * (at - 1))
                    for j in range(GROUP):
                        last = nc.tensor.matmul(ps[0:D, 6 + slot % 2, j * P:(j + 1) * P], ends[:, slot % 2, j, :],
                                                onehot[:, slot, j, :], start=True, stop=True)
                    last.then_inc(picked, 1)
                if (c := step.item(0)):
                    at, slot, turn = c
                    wait(pe, gathered1[slot], (turn + 1) * 64)
                    wait(pe, scan_done, at - 1)
                    for j in range(GROUP):
                        last = nc.tensor.transpose(ps[0:D, slot % 2, j * P:(j + 1) * P],
                                                   rows[:, slot, j * ROW1 + D + 1:(j + 1) * ROW1], ident[:, :])
                    last.then_inc(turned, 1)
                if (c := step.item(1)):
                    at, slot, turn = c
                    wait(pe, scan_done, at + 1)
                    wait(pe, ends_done, at - 1)
                    for j in range(GROUP):
                        last = nc.tensor.transpose(ps[:, 2 + slot % 2, j * D:(j + 1) * D],
                                                   scanned[:, slot % 2, j * P:(j + 1) * P], ident[0:D, 0:D])
                    last.then_inc(turned_back, 1)
                if (c := step.item(0)):
                    at, slot, turn = c
                    wait(pe, onehot1_done, at + 1)
                    wait(pe, sums_added, GROUP * (at - 1))
                    for j in range(GROUP):
                        last = nc.tensor.matmul(ps[0:D + 1, 4 + slot % 2, j * P:(j + 1) * P],
                                                rows[:, slot, j * ROW1:j * ROW1 + D + 1],
                                                onehot[:, slot, j, :], start=True, stop=True)
                    last.then_inc(rows_summed, 1)
            walk_edges(pe, 2, edges1)

            pe.wait_ge(sums_added, ET)
            pe.wait_ge(maxima_added, ET)
            pe.wait_ge(update_kept, NCH)

            def outs(step):
                at, slot, turn = step.item()
                h = h_feat[0:D, bass.ds(at * CHUNK, CHUNK)]
                wait(pe, out_kept, at - 1)
                wait(pe, out2_kept, at - 1)
                nc.tensor.matmul(ps[0:D, 4 + slot, :], w_neigh[:, 1, :], max_feat[:, bass.ds(at * CHUNK, CHUNK)],
                                 start=True, stop=True)
                nc.tensor.matmul(ps[0:D, 2 + slot, :], w_self[:, 0, :], h, start=True, stop=False)
                wait(pe, out_mean, at + 1)
                nc.tensor.matmul(ps[0:D, 2 + slot, :], w_neigh[:, 0, :], mean_chunk[0:D, slot, :],
                                 start=False, stop=True).then_inc(out_products, 1)
            walk_nodes(pe, 0, outs)

            def finish(step):
                if (c := step.item(1)):
                    at, slot, turn = c
                    wait(pe, finish_summed, at + 1)
                    wait(pe, finish_evac, at - 1)
                    for j in range(4):
                        last = nc.tensor.transpose(ps[:, 6 + slot, j * D:(j + 1) * D],
                                                   summed_parts[0:D, slot, j * P:(j + 1) * P], ident[0:D, 0:D])
                    last.then_inc(finish_turned, 1)
            walk_nodes(pe, 1, finish)

        @block.vector
        def _(dve):
            nc.vector.memset(w_edge[:, :, :], 0.0).then_inc(edge_weights_zero, 1)
            nc.vector.memset(h_chunk[D:D + 1, :, :], 1.0).then_inc(cleared, 1)
            nc.vector.memset(u_chunk[D:D + 1, :, :], 1.0).then_inc(cleared, 1)
            nc.vector.memset(msg[:, :, :, D:D + 1], 1.0).then_inc(sums_zero, 1)

            def moments(of, to, slot, done, ready):
                hold(dve, dve_passed)
                for j in range(4):
                    nc.vector.bn_stats(stats[:, slot, j, :], of(j)).then_inc(done[0], 1)
                wait(dve, done[0], done[1])
                hold(dve, dve_passed)
                for j in range(4):
                    last = nc.vector.bn_aggr(to[:, slot, j, :], stats[:, slot, j, :])
                last.then_inc(ready, 1)

            def minus_mean_rstd(of, rstd, to, slot, done):
                nc.vector.scalar_tensor_tensor(out=to[:, slot, :], in0=of[:, slot, :, 0], scalar=-1.0,
                                               in1=rstd[:, slot, :], op0=ALU.mult, op1=ALU.mult).then_inc(done, 1)

            def node_tile(t, at, j):
                return t[:, bass.ds(at * 4 + j, 1), :].rearrange("p a f -> p (a f)")

            def prepare(step):
                if (c := step.item(0)):
                    at, slot, turn = c
                    wait(dve, prep_nmr, at - 1)
                    if isinstance(at, int):
                        for k, (first, _) in enumerate(X_PIECES):
                            if at == first:
                                dve.wait_ge(x_loaded[k], 16)
                    moments(lambda j: node_tile(x_nodes, at, j), mv, slot, (prep_bn_stats, 4 * at + 4), prep_stats)
                if (c := step.item(1)):
                    at, slot, turn = c
                    wait(dve, prep_rstd, at + 1)
                    wait(dve, prep_h, at - 1)
                    minus_mean_rstd(mv, rstd, nmr, slot, prep_nmr)
                if (c := step.item(2)):
                    at, slot, turn = c
                    wait(dve, prep_turned, at + 1)
                    wait(dve, prep_product, at - 1)
                    nc.vector.tensor_copy(h_chunk[0:D, slot, :], ps[0:D, slot, :]).then_inc(prep_copied, 1)
                    nc.vector.tensor_copy(h_nodes[:, bass.ds(at * 4, 4), :], h_tile[:, slot, :, :]).then_inc(prep_kept, 1)
                    wait(dve, prep_copied, at + 1)
                    nc.vector.tensor_copy(h_feat[0:D, bass.ds(at * CHUNK, CHUNK)], h_chunk[0:D, slot, :])\
                      .then_inc(prep_kept, 1)
            walk_nodes(dve, 2, prepare)

            dve.wait_ge(edges_loaded, 16 * N_EDGE_LOADS)
            nc.vector.tensor_tensor(same, row_dst, row_prev, ALU.is_equal).then_inc(same_made, 1)
            nc.vector.tensor_copy(dst_rel[:, :], dst_i[:, :]).then_inc(dst_float, 1)
            nc.vector.tensor_tensor(is_end[:, :], dst_i[:, :], next_i, ALU.not_equal).then_inc(dst_float, 1)
            dve.wait_ge(columns_made, 2)
            nc.vector.tensor_scalar(lane[:, :], lane[:, :], float(P - 1), None, ALU.is_ge).then_inc(dst_float, 1)
            dve.wait_ge(dst_float, 3)
            nc.vector.tensor_scalar(is_end[:, :], is_end[:, :], lane[:, 0:1], None, ALU.max).then_inc(dst_ready, 1)
            dve.wait_ge(base_spread, 1)
            half = ET // 2
            for k in range(2):
                nc.vector.tensor_tensor(dst_rel[:, k * half:(k + 1) * half], dst_rel[:, k * half:(k + 1) * half],
                                        ps[:, 6 + k, 0:half], ALU.subtract).then_inc(dst_ready, 1)
            nc.vector.memset(sum_feat[:, :], 0.0).then_inc(sums_zero, 1)

            dve.wait_ge(edge_weights_loaded, 16 * N_EDGE_WEIGHTS)
            dve.wait_ge(m2_turned, 1)
            nc.vector.tensor_copy(w_m2t[:, 0:D], ps[0:D, 6, 0:D]).then_inc(m2_copied, 1)
            nc.vector.tensor_scalar(b_gate[:, :], b_gate[:, :], 0.5, None, ALU.mult).then_inc(u1_ready, 1)
            dve.wait_ge(u1_product, 1)
            nc.vector.tensor_copy(w_u1_sum[:, :], ps[0:D + 1, 7, 0:D]).then_inc(u1_ready, 1)
            dve.wait_ge(sums_zero, 2)
            dve.wait_ge(same_stored, 16)

            def bases(at):
                return nc.values_load_multi_w_load_instructions(
                    dst_i[0:1, bass.ds(at * GROUP, GROUP)], engines=[mybir.EngineType.DVE], min_val=0, max_val=N,
                    skip_runtime_bounds_check_because="destinations are node numbers, the padding's is N")[1]

            def edges0(step):
                if (c := step.item(1)):
                    at, slot, turn = c
                    wait(dve, gate_gelu, at + 1)
                    wait(dve, tanh_done, at - 1)
                    for j in range(GROUP):
                        last = nc.vector.tensor_tensor_reduce(
                            out=gate_act[:, slot % 2, j, :], in0=gate_act[:, slot % 2, j, :], in1=w_gate[:, :],
                            scale=1.0, scalar=0.0, op0=ALU.mult, op1=ALU.add, accum_out=logit[:, slot % 2, j:j + 1])
                    last.then_inc(logits_done, 1)
                if (c := step.item(0)):
                    at, slot, turn = c
                    wait(dve, gathered[slot], (turn + 1) * 64)
                    wait(dve, pre_product, at + 1)
                    wait(dve, msg_gelu, at - 1)
                    nc.vector.tensor_tensor(pre[:, slot % 2, :].rearrange("p (b f) -> p b f", b=2),
                                            rows0(slot).rearrange("p (b f) -> p b f", b=2),
                                            ps[:, 2 * (slot % 2):2 * (slot % 2) + 2, 0:2 * ROW0], ALU.add)\
                      .then_inc(pre_added, 1)
                one, three = step.item(1), step.item(3)
                if one:
                    at, slot, turn = one
                    wait(dve, tanh_done, at + 1)
                    wait(dve, summed, at - 1)
                    nc.vector.tensor_scalar(gate[:, slot % 2, :], tanh[:, slot % 2, :], 0.5, 0.5, ALU.mult, ALU.add)\
                      .then_inc(gate_done, 1)
                if three:
                    wait(dve, summed, three[0] + 1)
                    base = bases(three[0])
                if one:
                    wait(dve, gate_done, one[0] + 1)
                for j in range(GROUP):
                    if one:
                        at, slot, turn = one
                        last = nc.vector.tensor_scalar(onehot[:, slot % 2, j, :], columns[:, :],
                                                       dst_rel[:, bass.ds(at * GROUP + j, 1)],
                                                       gate[:, slot % 2, j:j + 1], ALU.is_equal, ALU.mult)
                        if j == GROUP - 1:
                            last.then_inc(onehot_done, 1)
                    if three:
                        at, slot, turn = three
                        window = sum_feat[:, bass.ds(base[j], P)]
                        wait(dve, window_added, at * GROUP + j)
                        nc.vector.tensor_tensor(window, window, ps[0:D + 1, 4 + slot % 2, j * P:(j + 1) * P], ALU.add)\
                          .then_inc(window_added, 1)
            walk_edges(dve, 3, edges0)

            def update(step):
                if (c := step.item(4)):
                    at, slot, turn = c
                    wait(dve, update_rstd2, at + 1)
                    wait(dve, update_h_rows, at - 1)
                    minus_mean_rstd(mv2, rstd2, nmr2, slot % 2, update_nmr2)
                if (c := step.item(3)):
                    at, slot, turn = c
                    chunk = x_nodes[:, bass.ds(at * 4, 4), :]
                    wait(dve, update_scaled, at + 1)
                    nc.vector.tensor_tensor(chunk, chunk, y_tile[:, slot % 2, :, :], ALU.add)\
                      .then_inc(update_x_added, 1)
                    wait(dve, update_x_added, at + 1)
                    moments(lambda j: node_tile(x_nodes, at, j), mv2, slot % 2, (update_bn_stats2, 4 * at + 4), update_stats2)
                if (c := step.item(2)):
                    at, slot, turn = c
                    wait(dve, update_rstd, at + 1)
                    wait(dve, update_normalized, at - 1)
                    minus_mean_rstd(mv, rstd, nmr, slot % 2, update_nmr)
                if (c := step.item(5)):
                    at, slot, turn = c
                    wait(dve, update_turned, at + 1)
                    wait(dve, update_pooled, at - 1)
                    nc.vector.tensor_copy(h_chunk[0:D, slot % 2, :], ps[0:D, 4 + slot % 2, :]).then_inc(update_copied, 1)
                if (c := step.item(1)):
                    at, slot, turn = c
                    wait(dve, update_product, at + 1)
                    wait(dve, update_normalized, at - 1)
                    nc.vector.tensor_tensor(h_tile[:, slot % 2, :, :], ps[:, 2 + slot % 2, 0:4 * D]
                                            .rearrange("p (t f) -> p t f", f=D),
                                            h_nodes[:, bass.ds(at * 4, 4), :], ALU.add).then_inc(update_residual, 1)
                    wait(dve, update_residual, at + 1)
                    moments(lambda j: h_tile[:, slot % 2, j, :], mv, slot % 2, (update_bn_stats, 4 * at + 4), update_stats)
            nc.vector.memset(max_feat[:, :], 0.0).then_inc(maxima_zero, 1)
            for j in range(GROUP):
                nc.vector.memset(out_rows[:, :, j * ROW1 + D:j * ROW1 + D + 1], 1.0).then_inc(ones_made, 1)
            dve.wait_ge(node_weights_loaded, 16 * N_NODE_WEIGHTS)
            dve.wait_ge(prep_kept, 2 * NCH)
            dve.wait_ge(prep_shifted, NCH)
            walk(dve, NCH, 5, RING, 2 * RING, update)

            dve.wait_ge(update_hidden, NCH)
            nc.vector.memset(sum_feat[:, :], 0.0).then_inc(sums_cleared, 1)
            dve.wait_ge(sums_cleared, 1)
            dve.wait_ge(maxima_zero, 1)

            def edges1(step):
                zero, one, three = step.item(0), step.item(1), step.item(3)
                if one:
                    sum_base = bases(one[0])
                if three:
                    max_base = bases(three[0])
                if zero:
                    wait(dve, picked, zero[0] - RING + 1)
                if one:
                    wait(dve, rows_summed, one[0] + 1)
                if three:
                    wait(dve, picked, three[0] + 1)
                for j in range(GROUP):
                    if zero:
                        at, slot, turn = zero
                        last = nc.vector.tensor_scalar(onehot[:, slot, j, :], columns[:, :],
                                                       dst_rel[:, bass.ds(at * GROUP + j, 1)], None, ALU.is_equal)
                        if j == GROUP - 1:
                            last.then_inc(onehot1_done, 1)
                    if one:
                        at, slot, turn = one
                        window = sum_feat[:, bass.ds(sum_base[j], P)]
                        wait(dve, sums_added, at * GROUP + j)
                        nc.vector.tensor_tensor(window, window, ps[0:D + 1, 4 + slot % 2, j * P:(j + 1) * P], ALU.add)\
                          .then_inc(sums_added, 1)
                    if three:
                        at, slot, turn = three
                        window = max_feat[:, bass.ds(max_base[j], P)]
                        wait(dve, maxima_added, at * GROUP + j)
                        nc.vector.tensor_tensor(window, window, ps[0:D, 6 + slot % 2, j * P:(j + 1) * P], ALU.max)\
                          .then_inc(maxima_added, 1)
                if zero:
                    at, slot, turn = zero
                    wait(dve, turned, at + 1)
                    wait(dve, mask_loaded[slot], (turn + 1) * 16)
                    wait(dve, turned_back, at - 1)
                    nc.vector.tensor_tensor_scan(scanned[:, slot % 2, :], stream[0:D, slot, :], ps[0:D, slot % 2, :],
                                                 0.0, ALU.mult, ALU.max).then_inc(scan_done, 1)
            walk_edges(dve, 3, edges1)

            dve.wait_ge(degree_moved, 16)
            nc.vector.tensor_scalar(degree[:, :], degree[:, :], 1.0, None, ALU.max).then_inc(degree_inverted, 1)
            dve.wait_ge(degree_inverted, 1)
            nc.vector.reciprocal(degree[:, :], degree[:, :]).then_inc(degree_inverted, 1)

            def outs(step):
                if (c := step.item(0)):
                    at, slot, turn = c
                    wait(dve, inverse_loaded[slot], (turn + 1) * 16)
                    wait(dve, out_products, at - 1)
                    nc.vector.tensor_tensor(mean_chunk[0:D, slot, :], sum_feat[0:D, bass.ds(at * CHUNK, CHUNK)],
                                            stream[0:D, slot, :], ALU.mult).then_inc(out_mean, 1)
                if (c := step.item(2)):
                    at, slot, turn = c
                    chunk = bass.ds(at * CHUNK, CHUNK)
                    wait(dve, out_products, at + 1)
                    nc.vector.tensor_tensor(max_feat[:, chunk], ps[0:D, 4 + slot, :], self_feat[0:D, chunk], ALU.add)\
                      .then_inc(out2_kept, 1)
                    wait(dve, out_kept, at + 1)
                    wait(dve, out2_kept, at + 1)
                    hold(dve, dve_passed)
                    width = LAST if isinstance(at, int) and at == NCH - 1 else CHUNK
                    for k, kept in enumerate((sum_feat, max_feat)):
                        nc.vector.bn_stats(bn_stats[:, k, bass.ds(at, 1), :].rearrange("p a f -> p (a f)"),
                                           kept[0:D, bass.ds(at * CHUNK, width)]).then_inc(out_stats, 1)
            walk_nodes(dve, 2, outs)

            dve.wait_ge(out_stats, 2 * NCH)
            for k in range(2):
                nc.vector.bn_aggr(bn_mv[:, k, :], bn_stats[:, k, :, :]).then_inc(norm_coefficients, 1)
            dve.wait_ge(norm_coefficients, 2)
            dve.wait_ge(norm_rstd, 2)
            nc.vector.tensor_tensor(bn_a[:, :], bn_scale[:, :], bn_rstd[:, :], ALU.mult).then_inc(norm_coefficients, 1)
            dve.wait_ge(norm_coefficients, 3)
            nc.vector.tensor_tensor(bn_am[:, :], bn_a[:, :], bn_mv[:, :, 0], ALU.mult).then_inc(norm_coefficients, 1)
            dve.wait_ge(norm_coefficients, 4)
            nc.vector.tensor_tensor(bn_am[:, :], bn_shift[:, :], bn_am[:, :], ALU.subtract).then_inc(norm_coefficients, 1)
            dve.wait_ge(norm_coefficients, 5)
            nc.vector.tensor_tensor(bn_c[:, 2:3], bn_am[:, 0:1], bn_am[:, 1:2], ALU.add).then_inc(norm_coefficients, 1)
            dve.wait_ge(out_kept, NCH)

            def finish(step):
                if (c := step.item(1)):
                    at, slot, turn = c
                    wait(dve, finish_scaled1, at + 1)
                    wait(dve, finish_turned, at - 1)
                    nc.vector.scalar_tensor_tensor(out=summed_parts[0:D, slot, :],
                                                   in0=max_feat[:, bass.ds(at * CHUNK, CHUNK)], scalar=bn_a[:, 1:2],
                                                   in1=scaled1[0:D, slot, :], op0=ALU.mult, op1=ALU.add)\
                      .then_inc(finish_summed, 1)
                if (c := step.item(3)):
                    at, slot, turn = c
                    wait(dve, finish_evac, at + 1)
                    y = y_tile[:, slot, :, :]
                    nc.vector.scalar_tensor_tensor(out=y, in0=y, scalar=0.01, in1=y, op0=ALU.mult, op1=ALU.max)\
                      .then_inc(finish_leaky, 1)
            walk_nodes(dve, 3, finish)


_WEIGHTS = ["L0_gnn_mW1", "L0_gnn_mb1", "L0_gnn_mW2", "L0_gnn_mb2", "L0_gnn_gW1", "L0_gnn_gb1", "L0_gnn_gW2",
            "L0_gnn_gb2", "L0_gnn_uW1", "L0_gnn_ub1", "L0_gnn_uW2", "L0_gnn_ub2", "L0_gnn_ln_g", "L0_gnn_ln_b",
            "L1_gnn_W_self1", "L1_gnn_W_neigh1", "L1_gnn_W_pool", "L1_gnn_b_pool", "L1_gnn_W_self2",
            "L1_gnn_W_neigh2", "L1_gnn_g1", "L1_gnn_beta1", "L1_gnn_g2", "L1_gnn_beta2"]


def kernel(**inputs):
    import numpy as _np
    import concourse.bacc as _bacc
    from concourse import mybir as _mybir
    from concourse.bass_utils import run_bass_kernel_spmd as _run

    def lanes(v):
        return v.reshape(ET, P).T

    src = _np.pad(_np.asarray(inputs["src"]), (0, EPAD - E))
    dst = _np.pad(_np.asarray(inputs["dst"]), (1, EPAD - E + 1), constant_values=(-1, N))
    laid = {
        "x": _np.pad(_np.asarray(inputs["x"]), ((0, NPAD - N), (0, 0))).reshape(NT, P, D).transpose(1, 0, 2),
        "src_lanes": lanes(src),
        "dst_lanes": lanes(dst[1:EPAD + 1]),
        "dst_next_lanes": lanes(dst[2:EPAD + 2]),
        "dst_ext": dst[0:EPAD + 1],
        "edge_attr_t": _np.pad(_np.asarray(inputs["edge_attr_32"]), ((0, EPAD - E), (0, 0)))
                          .reshape(NG, GROUP, P, DE).transpose(1, 3, 0, 2).reshape(GROUP * DE, NG * P),
    }
    for name in _WEIGHTS:
        laid[name] = _np.asarray(inputs[name])
    nc = _bacc.Bacc("TRN2", target_bir_lowering=False, num_devices=1)
    arrays, args = {}, []
    for name, a in laid.items():
        a = _np.ascontiguousarray(a)
        arrays[f"in_{name}"] = a
        args.append(nc.dram_tensor(f"in_{name}", a.shape, _mybir.dt.from_np(a.dtype), kind="ExternalInput").ap())
    args.append(nc.dram_tensor("out_0", (P, NT, D), _mybir.dt.float32, kind="ExternalOutput").ap())
    gnn(nc, *args)
    r = _run(nc, [arrays], core_ids=[0])
    return r.results[0]["out_0"].transpose(1, 0, 2).reshape(NPAD, D)[0:N]
```
